# Optimizing a Trainium2 kernel written in Bass

```python
import numpy as np
import jax
import jax.numpy as jnp

def _softmax(x, axis=-1):
    return jax.nn.softmax(x, axis=axis)

def _gelu(x):
    return jax.nn.gelu(x, approximate=True)

def _silu(x):
    return jax.nn.silu(x)

def _sigmoid(x):
    return jax.nn.sigmoid(x)

def _layernorm(x, axis=-1, eps=1e-05):
    m = jnp.mean(x, axis=axis, keepdims=True)
    v = jnp.var(x, axis=axis, keepdims=True)
    return (x - m) / jnp.sqrt(v + eps)

def _scatter_add(tgt, idx, src, axis=0):
    return tgt.at[idx].add(src)

def _segment_sum(src, seg, n):
    return jax.ops.segment_sum(src, seg, n)
kernel_name = 'mk_xattn_ffn_d1_seqx_r4_b2c8f8'

def setup_inputs(seed: int=0):
    np.random.seed(seed)
    _w = jnp.asarray

    def _rec_inputs():
        import jax
        import jax.numpy as jnp
        _rk = jax.random.key(seed)
        x = 7.22e-05 + 1 * jax.random.normal(jax.random.fold_in(_rk, 1), (16, 128, 512), jnp.float32)
        _lenS = 128 - jax.random.randint(jax.random.fold_in(_rk, 7), (16,), 0, max(1, 128 // 4) + 1, jnp.int32)
        _lenS2 = 128 - jax.random.randint(jax.random.fold_in(_rk, 8), (16,), 0, max(1, 128 // 4) + 1, jnp.int32)
        _ctx_1024P = jax.random.normal(jax.random.fold_in(_rk, 11), (16, 16, 256), jnp.float32)
        _ctx_1024c = jax.random.dirichlet(jax.random.fold_in(_rk, 511), 0.3 * jnp.ones((16,), jnp.float32), (16, 128))
        _ctx_1024t = jnp.einsum('bsk,bkd->bsd', _ctx_1024c, _ctx_1024P)
        _ctx_1024t = _ctx_1024t * jax.lax.rsqrt(jnp.mean(jnp.square(_ctx_1024t)) + 1e-12) * 0.953939
        ctx_1024 = -1.39393e-06 + 0.999914 * (_ctx_1024t + 0.3 * jax.random.normal(jax.random.fold_in(_rk, 611), (16, 128, 256), jnp.float32))
        fside_BxSx2_0 = jax.random.uniform(jax.random.fold_in(_rk, 12), (16, 128, 2), jnp.float32, 0.0, 0.999707)
        return (x, ctx_1024, fside_BxSx2_0)
    x, ctx_1024, fside_BxSx2_0 = _rec_inputs()

    def _L0_xattn_setup():
        import jax, jax.numpy as jnp
        import numpy as np
        DIM = 512
        CTX_DIM = 256
        N_HEADS = 32
        HEAD_DIM = DIM // N_HEADS
        POS_DIM = 2
        B, N, CTXN = (2, 512, 512)
        ROPE_BASE = 10000.0

        def apply_axial_rope(x, pos):
            b, n, h, d = x.shape
            p = pos.shape[-1]
            dpa = d // p
            half = dpa // 2
            freqs = ROPE_BASE ** (-jnp.arange(half, dtype=x.dtype) / half)
            ang = pos[..., :, None] * freqs
            cos = jnp.cos(ang)[:, :, None, :, :]
            sin = jnp.sin(ang)[:, :, None, :, :]
            xr = x.reshape(b, n, h, p, half, 2)
            x1, x2 = (xr[..., 0], xr[..., 1])
            out = jnp.stack([x1 * cos - x2 * sin, x1 * sin + x2 * cos], axis=-1)
            return out.reshape(b, n, h, d)
        key = jax.random.key(seed)
        ks = jax.random.split(key, 8)
        x = jax.random.normal(ks[0], (B, N, DIM), jnp.float32)
        ctx = jax.random.normal(ks[1], (B, CTXN, CTX_DIM), jnp.float32)
        pos_map = jax.random.uniform(ks[2], (B, N, POS_DIM), jnp.float32)
        ctx_pos_map = jax.random.uniform(ks[3], (B, CTXN, POS_DIM), jnp.float32)
        Wq = jax.random.normal(ks[4], (DIM, DIM), jnp.float32) / np.sqrt(DIM)
        Wkv = jax.random.normal(ks[5], (CTX_DIM, 2 * DIM), jnp.float32) / np.sqrt(CTX_DIM)
        Wout = jax.random.normal(ks[6], (DIM, DIM), jnp.float32) / np.sqrt(DIM)
        bout = jnp.zeros((DIM,), jnp.float32)
        return {'x': x, 'ctx': ctx, 'pos_map': pos_map, 'ctx_pos_map': ctx_pos_map, 'Wq': Wq, 'Wkv': Wkv, 'Wout': Wout, 'bout': bout}
    _L0_xattn_all = _L0_xattn_setup()
    _L0_xattn_in = {k: v for k, v in _L0_xattn_all.items() if k in ('Wq', 'Wkv', 'Wout', 'bout')}
    del _L0_xattn_all

    def _L0_ffn_setup():
        import jax, jax.numpy as jnp
        import numpy as np
        N_ACTIVE = 32
        key = jax.random.key(seed)
        ks = jax.random.split(key, 6)
        B, T, D, G, GD = (4, 512, 512, 1024, 64)
        x = jax.random.normal(ks[0], (B, T, D), jnp.float32)
        Wc = jax.random.normal(ks[1], (G, D), jnp.float32) * D ** (-0.5)
        temperature = jnp.array(1.0, jnp.float32)
        genes = jax.random.normal(ks[2], (G, GD), jnp.float32) * 0.02
        Wd = jax.random.normal(ks[3], (D, GD), jnp.float32) * GD ** (-0.5)
        Wu = jax.random.normal(ks[4], (D, GD), jnp.float32) * 0.02
        norm_w = jnp.ones((D,), jnp.float32)
        scale = jnp.array(0.1, jnp.float32)
        return {'x': x, 'Wc': Wc, 'temperature': temperature, 'genes': genes, 'Wd': Wd, 'Wu': Wu, 'norm_w': norm_w, 'scale': scale}
    _L0_ffn_all = _L0_ffn_setup()
    _L0_ffn_in = {k: v for k, v in _L0_ffn_all.items() if k in ('Wc', 'temperature', 'genes', 'Wd', 'Wu', 'norm_w', 'scale')}
    del _L0_ffn_all
    return {'x': x, 'ctx_1024': ctx_1024, 'fside_BxSx2_0': fside_BxSx2_0, 'L0_xattn_Wq': _L0_xattn_in['Wq'], 'L0_xattn_Wkv': _L0_xattn_in['Wkv'], 'L0_xattn_Wout': _L0_xattn_in['Wout'], 'L0_xattn_bout': _L0_xattn_in['bout'], 'L0_ffn_Wc': _L0_ffn_in['Wc'], 'L0_ffn_temperature': _L0_ffn_in['temperature'], 'L0_ffn_genes': _L0_ffn_in['genes'], 'L0_ffn_Wd': _L0_ffn_in['Wd'], 'L0_ffn_Wu': _L0_ffn_in['Wu'], 'L0_ffn_norm_w': _L0_ffn_in['norm_w'], 'L0_ffn_scale': _L0_ffn_in['scale']}

def reference(x, ctx_1024, fside_BxSx2_0, L0_xattn_Wq, L0_xattn_Wkv, L0_xattn_Wout, L0_xattn_bout, L0_ffn_Wc, L0_ffn_temperature, L0_ffn_genes, L0_ffn_Wd, L0_ffn_Wu, L0_ffn_norm_w, L0_ffn_scale):
    import jax
    import jax.numpy as jnp

    def _L0_xattn_ref(x, ctx, pos_map, ctx_pos_map, Wq, Wkv, Wout, bout):
        import jax, jax.numpy as jnp
        import numpy as np
        DIM = 512
        CTX_DIM = 256
        N_HEADS = 32
        HEAD_DIM = DIM // N_HEADS
        POS_DIM = 2
        B, N, CTXN = (2, 512, 512)
        ROPE_BASE = 10000.0

        def apply_axial_rope(x, pos):
            b, n, h, d = x.shape
            p = pos.shape[-1]
            dpa = d // p
            half = dpa // 2
            freqs = ROPE_BASE ** (-jnp.arange(half, dtype=x.dtype) / half)
            ang = pos[..., :, None] * freqs
            cos = jnp.cos(ang)[:, :, None, :, :]
            sin = jnp.sin(ang)[:, :, None, :, :]
            xr = x.reshape(b, n, h, p, half, 2)
            x1, x2 = (xr[..., 0], xr[..., 1])
            out = jnp.stack([x1 * cos - x2 * sin, x1 * sin + x2 * cos], axis=-1)
            return out.reshape(b, n, h, d)
        b, n, _ = x.shape
        ctx_n = ctx.shape[1]
        q = (x @ Wq).reshape(b, n, N_HEADS, HEAD_DIM)
        k, v = jnp.split(ctx @ Wkv, 2, axis=-1)
        k = k.reshape(b, ctx_n, N_HEADS, HEAD_DIM)
        v = v.reshape(b, ctx_n, N_HEADS, HEAD_DIM)
        q = apply_axial_rope(q, pos_map)
        k = apply_axial_rope(k, ctx_pos_map)
        scale = 1.0 / np.sqrt(HEAD_DIM).astype(np.float32)
        logits = jnp.einsum('bqhd,bkhd->bhqk', q, k) * scale
        w = jax.nn.softmax(logits, axis=-1)
        attn = jnp.einsum('bhqk,bkhd->bqhd', w, v)
        attn = attn.reshape(b, n, N_HEADS * HEAD_DIM)
        return attn @ Wout + bout

    def _L0_ffn_ref(x, Wc, temperature, genes, Wd, Wu, norm_w, scale):
        import jax, jax.numpy as jnp
        import numpy as np
        N_ACTIVE = 32
        eps = jnp.finfo(x.dtype).eps
        xn = x * jax.lax.rsqrt(jnp.mean(x * x, axis=-1, keepdims=True) + eps) * norm_w
        logits = jnp.einsum('btd,gd->btg', xn, Wc) / jnp.clip(temperature, 0.1)
        top_vals, top_idx = jax.lax.top_k(logits, N_ACTIVE)
        expr_w = jax.nn.softmax(top_vals, axis=-1)
        expressed = jnp.einsum('btk,btkc->btc', expr_w, genes[top_idx])
        down = jnp.tanh(jnp.einsum('btc,dc->btd', expressed, Wd))
        up = jnp.einsum('btc,dc->btd', expressed, Wu)
        return down * xn * up * scale
    x = x + _L0_xattn_ref(_layernorm(x, axis=-1), ctx_1024, fside_BxSx2_0, fside_BxSx2_0, L0_xattn_Wq, L0_xattn_Wkv, L0_xattn_Wout, L0_xattn_bout)
    x = x + _L0_ffn_ref(_layernorm(x, axis=-1), L0_ffn_Wc, L0_ffn_temperature, L0_ffn_genes, L0_ffn_Wd, L0_ffn_Wu, L0_ffn_norm_w, L0_ffn_scale)
    return x

_drawn_inputs = setup_inputs


def setup_inputs(seed=0):
    import zlib

    import numpy as np

    out = dict(_drawn_inputs(seed))
    spreads = {'L0_xattn_bout': (0.0, 0.1), 'L0_ffn_norm_w': (1.0, 0.6)}
    factors = {'L0_ffn_Wc': 29.715, 'L0_ffn_genes': 28.03, 'L0_ffn_Wd': 27.683, 'L0_ffn_Wu': 27.892}
    for name, (base, spread) in spreads.items():
        noise = np.random.default_rng([zlib.crc32(name.encode()), seed]).standard_normal(out[name].shape)
        drawn = base * np.exp(spread * noise) if base else spread * noise
        out[name] = jnp.asarray(drawn.astype(out[name].dtype))
    for name, factor in factors.items():
        out[name] = (out[name] * factor).astype(out[name].dtype)
    return out
```

```python
from contextlib import ExitStack

import concourse.bass as bass
from concourse import mybir

P = 128
TILES = 16
DIM, CTX = 512, 256
HEADS, HD = 32, 16
GENES, GD = 1024, 64
TOP = 32
XK, CK, GK = DIM // P, CTX // P, GENES // P
XSLOTS = 4
GROUPS = 4
GH = HEADS // GROUPS
LN_EPS = 1e-5
RMS_EPS = 2.0 ** -23
REMOVED = -3.0e38
ROPE_FREQS = [10000.0 ** (-j / 4) for j in range(4)]
TWO_PI_HI, TWO_PI_LO = 6.28125, 6.283185307179586 - 6.28125

f32, f32r = mybir.dt.float32, mybir.dt.float32r
f16, bf16, i32 = mybir.dt.float16, mybir.dt.bfloat16, mybir.dt.int32
ALU = mybir.AluOpType
ACT = mybir.ActivationFunctionType


def build(nc, x, ctx, pos, wq, wkv, wout, bout, wc, temp, genes, wd, wu, norm_w, scale, out):
    stack = ExitStack()
    with stack:
        def sb(name, shape, dt=f32):
            return stack.enter_context(nc.sbuf_tensor(name, shape, dt))

        def ps(name):
            return stack.enter_context(nc.psum_tensor(name, [P, 1024], f32))

        def sem(name):
            return stack.enter_context(nc.semaphore(name))

        wq_h, wq_l = sb("wq_h", [P, XK, DIM], f32r), sb("wq_l", [P, XK, DIM], f32r)
        wkv_h, wkv_l = sb("wkv_h", [P, CK, 2 * DIM], f32r), sb("wkv_l", [P, CK, 2 * DIM], f32r)
        wout_h, wout_l = sb("wout_h", [P, XK, DIM], f32r), sb("wout_l", [P, XK, DIM], f32r)
        wcT_h, wcT_l = sb("wcT_h", [P, XK, GENES], f32r), sb("wcT_l", [P, XK, GENES], f32r)
        wduT_h, wduT_l = sb("wduT_h", [2 * GD, 2 * DIM], f32r), sb("wduT_l", [GD, 2 * DIM], f32r)
        genes_sb = sb("genes_sb", [P, GK, GD])
        bout_sb = sb("bout_sb", [P, DIM])
        du_raw = sb("du_raw", [P, 2, XK, 2 * GD])
        norm_sb = sb("norm_sb", [P, XK])
        wc_scale = sb("wc_scale", [P, XK])
        up_scale = sb("up_scale", [P, XK])
        knob = sb("knob", [P, 4])
        minus_half = sb("minus_half", [P, 1])
        ident = sb("ident", [P, P])
        ident16 = sb("ident16", [P, P], f16)
        identb = sb("identb", [P, P], bf16)
        pick = sb("pick", [P, HEADS])
        select = sb("select", [P, HEADS, P], bf16)
        pos_sb = sb("pos_sb", [P, TILES, 2])
        cos_t, sin_t = sb("cos_t", [P, TILES * 8]), sb("sin_t", [P, TILES * 8])
        turns = sb("turns", [P, TILES * 8], i32)
        angle = sb("angle", [P, 3, TILES * 8])

        stage_a = sb("stage_a", [P, 4096])
        stage_b = sb("stage_b", [P, 6144])
        wc_raw = stage_a[:, :].rearrange("p (g d) -> p g d", d=DIM)
        wq_raw = stage_b[:, 0:2048]
        wkv_raw = stage_b[:, 2048:4096]
        wout_raw = stage_b[:, 4096:6144]
        probs = [stage_a[:, 0:1024], stage_a[:, 1024:2048]]
        gene_w = stage_a[:, 2048:3072]
        gene_wT = stage_a[:, 3072:4096]
        qk_sb = stage_b[:, 0:1024]
        qk_cos, qk_sin = stage_b[:, 1024:2048], stage_b[:, 2048:3072]
        logit = stage_b[:, 3072:4096]
        rest = stage_b[:, 4096:5120]
        oT_sb = stage_b[:, 5120:6144]

        x_ring = sb("x_ring", [P, XSLOTS * DIM])
        ctx_sb = sb("ctx_sb", [P, CTX])
        xn = sb("xn", [P, DIM])
        xT_h, xT_l = sb("xT_h", [P, DIM], f32r), sb("xT_l", [P, DIM], f32r)
        cT_h, cT_l = sb("cT_h", [P, CTX], f32r), sb("cT_l", [P, CTX], f32r)
        turned = sb("turned", [P, 2 * DIM])
        parts = sb("parts", [P, 2 * HEADS, 4, HD], f16)
        qT, kT = sb("qT", [P, HEADS // 2 * P], f16), sb("kT", [P, HEADS // 2 * P], f16)
        v_ext = sb("v_ext", [P, HEADS, 32])
        attn = sb("attn", [P, DIM])
        aT_h, aT_l = sb("aT_h", [P, DIM], f32r), sb("aT_l", [P, DIM], f32r)
        yn = sb("yn", [P, DIM])
        yT_h, yT_l = sb("yT_h", [P, DIM], f32r), sb("yT_l", [P, DIM], f32r)
        down = sb("down", [P, DIM])
        row_max = sb("row_max", [P, HEADS])
        neg_max = sb("neg_max", [P, 4 * HEADS], bf16)
        neg_maxT = sb("neg_maxT", [P, P], bf16)
        inv_sum = sb("inv_sum", [P, HEADS])
        bn1, bn2 = sb("bn1", [P, 6]), sb("bn2", [P, 6])
        mv1, mv2 = sb("mv1", [P, 2]), sb("mv2", [P, 2])
        var1, rstd1 = sb("var1", [P, 1]), sb("rstd1", [P, 1])
        var2, rstd2 = sb("var2", [P, 1]), sb("rstd2", [P, 1])
        normx = sb("normx", [P, 2])
        top = sb("top", [P, TOP])
        neg_top = sb("neg_top", [P, 1])
        gene_sum, inv_gene_sum = sb("gene_sum", [P, 1]), sb("inv_gene_sum", [P, 1])
        e_sb = sb("e_sb", [P, 2, GD])
        eT_h = sb("eT_h", [2 * GD, P], f32r)
        eT_hl = sb("eT_hl", [2 * GD, P], f32r)

        score_a, score_b, dense, gene = ps("score_a"), ps("score_b"), ps("dense"), ps("gene")

        s_wq, s_wkv, s_wout, s_wc, s_du, s_small = (sem(n) for n in (
            "wq_in", "wkv_in", "wout_in", "wc_in", "du_in", "small_in"))
        s_ident = sem("ident_ready")
        s_pool_setup = sem("pool_setup")
        s_setup = sem("dve_setup")
        s_act_setup = sem("act_setup")
        s_wcT = sem("wcT_in_psum")
        s_duT = sem("duT_in_psum")
        s_trig = sem("trig_ready")
        s_angle, s_scales, s_consts, s_up = (sem(n) for n in (
            "angles_ready", "scales_ready", "constants_ready", "up_weights_scaled"))
        s_split, s_split_wcT, s_split_duT = sem("weights_split"), sem("wcT_split"), sem("duT_split")
        s_wcT_h = sem("wcT_h_done")
        s_x, s_ctx = sem("x_loaded"), sem("ctx_loaded")
        s_bn1, s_mv1, s_var1, s_rstd1, s_xn = (sem(n) for n in (
            "bn1_done", "mv1_done", "var1_done", "rstd1_done", "xn_done"))
        s_xT, s_cT = sem("xT_in_psum"), sem("cT_in_psum")
        s_xT_h, s_xT_l, s_cT_h, s_cT_l = (sem(n) for n in ("xT_h_done", "xT_l_done", "cT_h_done", "cT_l_done"))
        s_q, s_k, s_v = sem("q_in_psum"), sem("k_in_psum"), sem("v_in_psum")
        s_q_sb, s_k_sb, s_v_sb = sem("q_read"), sem("k_read"), sem("v_read")
        s_cosm, s_sinm, s_rot1, s_rot = sem("qk_cos_done"), sem("qk_sin_done"), sem("rope_first"), sem("rope_done")
        s_hi, s_lo = sem("qk_hi_done"), sem("qk_lo_done")
        s_xb = sem("bout_added")
        s_tr = [sem(f"qkT{n}_in_psum") for n in range(4)]
        s_trr = [sem(f"qkT{n}_read") for n in range(4)]
        s_sc = [sem(f"scores{g}_in_psum") for g in range(GROUPS)]
        s_mx = [sem(f"max{g}_done") for g in range(GROUPS)]
        s_nmh, s_nml = sem("neg_max_hi_done"), sem("neg_max_lo_done")
        s_nmT, s_nmT_sb = sem("neg_maxT_in_psum"), sem("neg_maxT_read")
        s_st = [sem(f"scoresT{g}_in_psum") for g in range(GROUPS)]
        s_ex = [sem(f"exp{g}_done") for g in range(GROUPS)]
        s_av = [sem(f"values{g}_done") for g in range(GROUPS)]
        s_oT = [sem(f"oT{n}_read") for n in range(2)]
        s_o, s_inv, s_attn = sem("o_in_psum"), sem("inv_sum_done"), sem("attn_done")
        s_aT, s_aT_h, s_aT_l = sem("attnT_in_psum"), sem("attnT_h_done"), sem("attnT_l_done")
        s_proj, s_x1 = sem("proj_in_psum"), sem("x1_done")
        s_bn2, s_mv2, s_var2, s_norm2, s_yn = (sem(n) for n in (
            "bn2_done", "mv2_done", "var2_done", "norm2_done", "yn_done"))
        s_mean2 = sem("mean2_copied")
        s_yT, s_yT_h, s_yT_l = sem("ynT_in_psum"), sem("ynT_h_done"), sem("ynT_l_done")
        s_normx = sem("norm_copied")
        s_lg = [sem(f"logits{n}_in_psum") for n in range(2)]
        s_lgr = [sem(f"logits{n}_read") for n in range(2)]
        s_top = [sem(f"top{n}_found") for n in range(4)]
        s_rem = [sem(f"top{n}_removed") for n in range(4)]
        s_ntop, s_gexp, s_gw, s_ginv = (sem(n) for n in ("neg_top_done", "gene_exp_done", "gene_w_done", "inv_gene_sum_done"))
        s_wT = [sem(f"gene_wT{n}_in_psum") for n in range(2)]
        s_wTr = [sem(f"gene_wT{n}_read") for n in range(2)]
        s_e, s_e_sb, s_eT, s_eT_h, s_eT_l = (sem(n) for n in ("e_in_psum", "e_scaled", "eT_in_psum", "eT_h_done", "eT_l_done"))
        s_dn, s_upp, s_tanh, s_t1, s_t2, s_y = (sem(n) for n in (
            "down_in_psum", "up_in_psum", "tanh_done", "t1_done", "t2_done", "y_done"))
        s_out = sem("out_stored")

        def slot(t):
            if isinstance(t, int):
                return x_ring[:, (t % XSLOTS) * DIM:(t % XSLOTS + 1) * DIM]
            return x_ring[:, bass.ds((t % XSLOTS) * DIM, DIM)]

        def trig(table, t):
            at = table[:, t * 8:(t + 1) * 8] if isinstance(t, int) else table[:, bass.ds(t * 8, 8)]
            return at.unsqueeze(1).broadcast_to([P, 4 * HEADS, 8])

        q_parts, k_parts = parts[:, 0:HEADS], parts[:, HEADS:2 * HEADS]

        def head_major(t, n):
            return t[:, n * DIM:(n + 1) * DIM].rearrange("p (h d) -> p h d", d=HD)

        def pair_in(n, m):
            at = n * HEADS + 2 * m
            return parts[:, at:at + 2].rearrange("p h l d -> p (h l d)")

        def rows_of(t, head):
            r = 64 * (head % 2)
            return t[r:r + 64, (head // 2) * P:(head // 2 + 1) * P]

        score_of = [score_a, score_b, score_a, score_b]
        scoreT_of = [score_b, score_a, score_b, score_a]

        block = stack.enter_context(nc.Block())

        def first(t):
            return isinstance(t, int) and t == 0

        def hold(eng):
            eng.wait_ge(s_trig, 1)

        def run(eng, iteration):
            iteration(0, None, None)
            iteration(1, 0, None)
            iteration(2, 1, 0)
            with eng.Fori(3, TILES) as i:
                iteration(i, i - 1, i - 2)
            iteration(None, TILES - 1, TILES - 2)
            iteration(None, None, TILES - 1)

        @block.sync
        def _(sp):
            sp.dma_start(wc_raw, wc.rearrange("(g p) d -> p g d", p=P)).then_inc(s_wc, 16)
            for n, w in enumerate((wd, wu)):
                for half in range(2):
                    sp.dma_start(du_raw[:, n, :, half * GD:(half + 1) * GD],
                                 w.rearrange("(k p) c -> p k c", p=P)).then_inc(s_du, 16)

            def load_x(t):
                if isinstance(t, int):
                    src = x[t]
                else:
                    src = x[bass.ds(t, 1)].rearrange("o p n -> p (o n)")
                sp.dma_start(slot(t), src).then_inc(s_x, 16)

            def load_ctx(t):
                if isinstance(t, int):
                    src = ctx[t]
                else:
                    src = ctx[bass.ds(t, 1)].rearrange("o p n -> p (o n)")
                sp.dma_start(ctx_sb[:], src).then_inc(s_ctx, 16)

            def store(t):
                if isinstance(t, int):
                    dst = out[t]
                else:
                    dst = out[bass.ds(t, 1)].rearrange("o p n -> p (o n)")
                sp.dma_start(dst, slot(t)).then_inc(s_out, 16)

            load_x(0)
            load_ctx(0)

            def iteration(a, b, c):
                if a is not None and not (isinstance(a, int) and a == TILES - 1):
                    sp.wait_ge(s_x, (a + 1) * 16)
                    if not isinstance(a, int) or a > 2:
                        sp.wait_ge(s_out, (a - 2) * 16)
                    load_x(a + 1)
                    sp.wait_ge(s_cT, a + 1)
                    load_ctx(a + 1)
                if c is not None:
                    sp.wait_ge(s_y, c + 1)
                    store(c)

            iteration(0, None, None)
            iteration(1, 0, None)
            iteration(2, 1, 0)
            with sp.Fori(3, TILES - 1) as i:
                iteration(i, i - 1, i - 2)
            iteration(TILES - 1, TILES - 2, TILES - 3)
            iteration(None, TILES - 1, TILES - 2)
            iteration(None, None, TILES - 1)
            sp.wait_ge(s_out, TILES * 16)

        @block.gpsimd
        def _(pool):
            pool.memset(ident[:], 0.0).then_inc(s_pool_setup, 1)
            pool.wait_ge(s_pool_setup, 1)
            pool.affine_select(out=ident[:], in_=ident[:], compare_op=ALU.not_equal, fill=1.0, base=0,
                               pattern=[[-1, P]], channel_multiplier=1).then_inc(s_ident, 1)
            pool.memset(minus_half[:], -0.5).then_inc(s_pool_setup, 1)
            pool.wait_ge(s_pool_setup, 2)

            def ln1(t):
                pool.wait_ge(s_var1, t + 1)
                pool.tensor_tensor(rstd1[:], var1[:], minus_half[:], ALU.pow).then_inc(s_rstd1, 1)

            def add_bout(t):
                pool.wait_ge(s_xn, t + 1)
                pool.tensor_tensor(slot(t), slot(t), bout_sb[:], ALU.add).then_inc(s_xb, 1)

            def rope(t):
                src = qk_sb.rearrange("p (a j) -> p a j", j=8)
                pool.wait_ge(s_q_sb, t + 1)
                pool.wait_ge(s_k_sb, t + 1)
                if not first(t):
                    pool.wait_ge(s_rot, t)
                pool.tensor_tensor(qk_cos.rearrange("p (a j) -> p a j", j=8), src, trig(cos_t, t),
                                   ALU.mult).then_inc(s_cosm, 1)
                pool.tensor_tensor(qk_sin.rearrange("p (a j) -> p a j", j=8), src, trig(sin_t, t),
                                   ALU.mult).then_inc(s_sinm, 1)

            def rope_sum(t):
                c = qk_cos.rearrange("p (s two h j) -> p s two h j", s=2, two=2, j=8)
                s = qk_sin.rearrange("p (s two h j) -> p s two h j", s=2, two=2, j=8)
                o = turned[:].rearrange("p (h two j) -> p h two j", two=2, j=8)
                pool.wait_ge(s_cosm, t + 1)
                pool.wait_ge(s_sinm, t + 1)
                if not first(t):
                    pool.wait_ge(s_hi, t)
                    pool.wait_ge(s_lo, t)
                for n in range(2):
                    hs = slice(n * HEADS, (n + 1) * HEADS)
                    pool.tensor_tensor(o[:, hs, 0], c[:, n, 0], s[:, n, 1], ALU.subtract)
                    last = pool.tensor_tensor(o[:, hs, 1], c[:, n, 1], s[:, n, 0], ALU.add)
                last.then_inc(s_rot, 1)

            def split_lo(t):
                pool.wait_ge(s_rot, t + 1)
                pool.wait_ge(s_hi, t + 1)
                if not first(t):
                    pool.wait_ge(s_tr[3], t)
                pool.tensor_tensor(q_parts[:, :, 1], head_major(turned, 0), q_parts[:, :, 0], ALU.subtract)
                pool.tensor_tensor(k_parts[:, :, 2], head_major(turned, 1), k_parts[:, :, 0],
                                   ALU.subtract).then_inc(s_lo, 1)

            def ln2(t):
                pool.wait_ge(s_var2, t + 1)
                if not first(t):
                    pool.wait_ge(s_normx, t)
                pool.tensor_tensor(rstd2[:], var2[:], minus_half[:], ALU.pow).then_inc(s_norm2, 1)

            def finish(t):
                pool.wait_ge(s_t2, t + 1)
                pool.tensor_tensor(slot(t), slot(t), down[:], ALU.add).then_inc(s_y, 1)

            pool.wait_ge(s_small, 16 * 6)
            pool.wait_ge(s_trig, 1)

            def iteration(a, b, c):
                if a is not None:
                    ln1(a)
                    add_bout(a)
                    rope(a)
                    rope_sum(a)
                if b is not None:
                    ln2(b)
                if a is not None:
                    split_lo(a)
                if c is not None:
                    finish(c)

            run(pool, iteration)

        @block.scalar
        def _(act):
            act.dma_start(norm_sb[:], norm_w).then_inc(s_small, 16)
            act.dma_start(knob[:, 0:1], temp.rearrange("(o n) -> o n", o=1).broadcast_to([P, 1])).then_inc(s_small, 16)
            act.dma_start(knob[:, 1:2], scale.rearrange("(o n) -> o n", o=1).broadcast_to([P, 1])).then_inc(s_small, 16)
            act.dma_start(bout_sb[:], bout.rearrange("(o n) -> o n", o=1).broadcast_to([P, DIM])).then_inc(s_small, 16)
            act.dma_start(pos_sb[:], pos.rearrange("t p c -> p t c")).then_inc(s_small, 16)
            act.dma_start(genes_sb[:], genes.rearrange("(g p) c -> p g c", p=P)).then_inc(s_small, 16)
            act.dma_start(wq_raw, wq.rearrange("(k p) n -> p k n", p=P)).then_inc(s_wq, 16)
            act.dma_start(wkv_raw, wkv.rearrange("(k p) n -> p k n", p=P)).then_inc(s_wkv, 16)
            act.dma_start(wout_raw, wout.rearrange("(k p) n -> p k n", p=P)).then_inc(s_wout, 16)

            act.wait_ge(s_angle, 1)
            nc.scalar.activation(sin_t[:], angle[:, 0], ACT.Sin)
            nc.scalar.activation(cos_t[:], angle[:, 1], ACT.Sin).then_inc(s_trig, 1)

            act.wait_ge(s_wq, 16)
            for k in range(XK):
                nc.scalar.activation(
                    wq_h[:, k].rearrange("p (two a) -> p two a", two=2),
                    wq_raw[:, k * DIM:(k + 1) * DIM].rearrange("p (a two) -> p two a", two=2),
                    ACT.Copy, scale=0.25)
            act.wait_ge(s_wkv, 16)
            for k in range(CK):
                raw = wkv_raw[:, k * 1024:(k + 1) * 1024]
                nc.scalar.activation(wkv_h[:, k, 0:DIM].rearrange("p (two a) -> p two a", two=2),
                                     raw[:, 0:DIM].rearrange("p (a two) -> p two a", two=2), ACT.Copy)
                nc.scalar.activation(wkv_h[:, k, DIM:1024], raw[:, DIM:1024], ACT.Copy)
            act.wait_ge(s_wout, 16)
            nc.scalar.activation(wout_h[:].rearrange("p k n -> p (k n)"), wout_raw,
                                 ACT.Copy).then_inc(s_act_setup, 1)
            act.wait_ge(s_scales, 1)
            for k, bank in enumerate((score_a, score_b, dense, gene)):
                act.wait_ge(s_wcT, k + 1)
                last = nc.scalar.activation(wcT_h[:, k], bank[:], ACT.Copy, scale=wc_scale[:, k:k + 1])
                last.then_inc(s_wcT_h, 1)
            act.wait_ge(s_duT, 1)
            nc.scalar.activation(wduT_h[:], score_a[:], ACT.Copy).then_inc(s_act_setup, 1)

            def x_hi(t):
                act.wait_ge(s_xT, t + 1)
                if not first(t):
                    act.wait_ge(s_q, t)
                nc.scalar.activation(xT_h[:], dense[:, 0:DIM], ACT.Copy).then_inc(s_xT_h, 1)
                act.wait_ge(s_cT, t + 1)
                if not first(t):
                    act.wait_ge(s_v, t)
                nc.scalar.activation(cT_h[:], dense[:, 512:512 + CTX], ACT.Copy).then_inc(s_cT_h, 1)

            def read_q(t):
                act.wait_ge(s_q, t + 1)
                if not first(t):
                    act.wait_ge(s_sinm, t)
                nc.scalar.activation(qk_sb[:, 0:DIM], dense[:, 0:DIM], ACT.Copy).then_inc(s_q_sb, 1)

            def read_k(t):
                act.wait_ge(s_k, t + 1)
                nc.scalar.activation(qk_sb[:, DIM:2 * DIM], dense[:, 512:1024], ACT.Copy).then_inc(s_k_sb, 1)

            def read_v(t):
                act.wait_ge(s_v, t + 1)
                if not first(t):
                    act.wait_ge(s_av[3], t)
                nc.scalar.activation(v_ext[:, :, 0:HD], dense[:, 0:DIM].rearrange("p (h d) -> p h d", d=HD),
                                     ACT.Copy).then_inc(s_v_sb, 1)

            def split_hi(t):
                act.wait_ge(s_rot, t + 1)
                if not first(t):
                    act.wait_ge(s_tr[3], t)
                twice = [P, HEADS, 2, HD]
                nc.scalar.activation(q_parts[:, :, 0:3:2], head_major(turned, 0).unsqueeze(2).broadcast_to(twice),
                                     ACT.Copy)
                nc.scalar.activation(k_parts[:, :, 0:2], head_major(turned, 1).unsqueeze(2).broadcast_to(twice),
                                     ACT.Copy).then_inc(s_hi, 1)

            def read_qkT(t, n):
                act.wait_ge(s_tr[n], t + 1)
                if not first(t):
                    act.wait_ge(s_st[3], t)
                dst = (qT, qT, kT, kT)[n][:, (n % 2) * 1024:(n % 2 + 1) * 1024]
                src = dense[:, (n % 2) * 512:(n % 2 + 1) * 512].bitcast(f16)
                nc.scalar.activation(dst, src, ACT.Copy).then_inc(s_trr[n], 1)

            def read_neg_max(t):
                act.wait_ge(s_nmT, t + 1)
                if not first(t):
                    act.wait_ge(s_st[3], t)
                nc.scalar.activation(neg_maxT[:], score_a[:, 0:64].bitcast(bf16), ACT.Copy).then_inc(s_nmT_sb, 1)

            def exp_group(t, g):
                act.wait_ge(s_st[g], t + 1)
                if g >= 2:
                    act.wait_ge(s_av[g - 2], t + 1)
                elif not first(t):
                    act.wait_ge(s_av[g + 2], t)
                nc.scalar.activation(probs[g % 2], scoreT_of[g][:], ACT.Exp).then_inc(s_ex[g], 1)

            def read_oT(t, n):
                act.wait_ge(s_av[2 * n + 1], t + 1)
                if not first(t):
                    act.wait_ge(s_o, t)
                nc.scalar.activation(oT_sb[:, n * 512:(n + 1) * 512], dense[:, n * 512:(n + 1) * 512],
                                     ACT.Copy).then_inc(s_oT[n], 1)

            def attn_hi(t):
                act.wait_ge(s_aT, t + 1)
                if not first(t):
                    act.wait_ge(s_proj, t)
                nc.scalar.activation(aT_h[:], score_a[:, 0:DIM], ACT.Copy).then_inc(s_aT_h, 1)

            def y_hi(t):
                act.wait_ge(s_yT, t + 1)
                if not first(t):
                    act.wait_ge(s_lg[1], t)
                nc.scalar.activation(yT_h[:], score_a[:, 0:DIM], ACT.Copy).then_inc(s_yT_h, 1)

            def read_logits(t, n):
                act.wait_ge(s_lg[n], t + 1)
                if not first(t):
                    act.wait_ge(s_rem[0], t)
                    act.wait_ge(s_gexp, t)
                nc.scalar.activation(logit[:, n * 512:(n + 1) * 512], gene[:, n * 512:(n + 1) * 512],
                                     ACT.Copy).then_inc(s_lgr[n], 1)

            def gene_exp(t):
                act.wait_ge(s_ntop, t + 1)
                if not first(t):
                    act.wait_ge(s_wT[1], t)
                nc.scalar.activation(gene_w, logit, ACT.Exp, bias=neg_top[:]).then_inc(s_gexp, 1)

            def read_wT(t, n):
                act.wait_ge(s_wT[n], t + 1)
                if not first(t):
                    act.wait_ge(s_e, t)
                nc.scalar.activation(gene_wT[:, n * 512:(n + 1) * 512], gene[:, n * 512:(n + 1) * 512],
                                     ACT.Copy).then_inc(s_wTr[n], 1)

            def e_hi(t):
                act.wait_ge(s_eT, t + 1)
                if not first(t):
                    act.wait_ge(s_upp, t)
                nc.scalar.activation(eT_h[:], gene[:, 512:512 + P], ACT.Copy).then_inc(s_eT_h, 1)

            def tanh(t):
                act.wait_ge(s_dn, t + 1)
                if not first(t):
                    act.wait_ge(s_y, t)
                nc.scalar.activation(down[:], gene[:, 0:DIM], ACT.Tanh).then_inc(s_tanh, 1)

            def iteration(a, b, c):
                if c is not None:
                    read_logits(c, 0)
                if a is not None:
                    x_hi(a)
                if c is not None:
                    read_logits(c, 1)
                if a is not None:
                    read_q(a)
                if b is not None:
                    read_neg_max(b)
                if a is not None:
                    read_k(a)
                if c is not None:
                    gene_exp(c)
                if b is not None:
                    for g in range(GROUPS):
                        exp_group(b, g)
                        if g == 2:
                            read_oT(b, 0)
                    read_oT(b, 1)
                if a is not None:
                    read_v(a)
                if b is not None:
                    attn_hi(b)
                if a is not None:
                    split_hi(a)
                if c is not None:
                    read_wT(c, 0)
                    read_wT(c, 1)
                    e_hi(c)
                    tanh(c)
                if b is not None:
                    y_hi(b)
                if a is not None:
                    for n in range(4):
                        read_qkT(a, n)

            run(act, iteration)

        @block.vector
        def _(dve):
            steps = [0]

            def step(instruction):
                instruction.then_inc(s_setup, 1)
                steps[0] += 1
                dve.wait_ge(s_setup, steps[0])

            dve.wait_ge(s_small, 16 * 6)
            by_freq = angle[:, 0].rearrange("p (t j) -> p t j", j=4)
            for j, freq in enumerate(ROPE_FREQS):
                last = nc.vector.tensor_scalar(by_freq[:, :, j:j + 1],
                                               pos_sb[:].rearrange("p t (c o) -> p (t c) o", o=1),
                                               freq, None, ALU.mult)
            step(last)
            step(nc.vector.tensor_scalar(turns[:], angle[:, 0], 1.0 / (TWO_PI_HI + TWO_PI_LO), None, ALU.mult))
            step(nc.vector.scalar_tensor_tensor(angle[:, 0], turns[:], -TWO_PI_HI, angle[:, 0], ALU.mult, ALU.add))
            step(nc.vector.scalar_tensor_tensor(angle[:, 0], turns[:], -TWO_PI_LO, angle[:, 0], ALU.mult, ALU.add))
            step(nc.vector.tensor_scalar(angle[:, 0], angle[:, 0], 3.1415925, -3.1415925, ALU.min, ALU.max))
            step(nc.vector.tensor_scalar(angle[:, 2], angle[:, 0], -1.0, None, ALU.mult))
            step(nc.vector.tensor_tensor(angle[:, 1], angle[:, 0], angle[:, 2], ALU.max))
            nc.vector.tensor_scalar(angle[:, 1], angle[:, 1], -1.0, 1.5707963, ALU.mult, ALU.add).then_inc(s_angle, 1)

            step(nc.vector.tensor_scalar(knob[:, 2:3], knob[:, 0:1], 0.1, None, ALU.max))
            step(nc.vector.reciprocal(knob[:, 2:3], knob[:, 2:3]))
            nc.vector.tensor_scalar(wc_scale[:], norm_sb[:], knob[:, 2:3], None, ALU.mult)
            step(nc.vector.tensor_scalar(up_scale[:], norm_sb[:], knob[:, 1:2], None, ALU.mult))
            nc.vector.tensor_copy(knob[:, 3:4], knob[:, 2:3]).then_inc(s_scales, 1)
            dve.wait_ge(s_du, 64)
            nc.vector.tensor_tensor(du_raw[:, 1], du_raw[:, 1],
                                    up_scale[:].unsqueeze(2).broadcast_to([P, XK, 2 * GD]), ALU.mult).then_inc(s_up, 1)

            dve.wait_ge(s_ident, 1)
            nc.vector.tensor_copy(ident16[:], ident[:])
            nc.vector.tensor_copy(identb[:], ident[:])
            step(nc.vector.tensor_tensor(pick[:], ident[:, 0:32], ident[:, 32:64], ALU.add))
            step(nc.vector.tensor_tensor(pick[:], pick[:], ident[:, 64:96], ALU.add))
            step(nc.vector.tensor_tensor(pick[:], pick[:], ident[:, 96:128], ALU.add))
            nc.vector.tensor_copy(select[:], pick[:].unsqueeze(2).broadcast_to([P, HEADS, P]))
            nc.vector.memset(v_ext[:, :, HD:32], 0.0)
            step(nc.vector.memset(parts[:, :, 3], 0.0))
            nc.vector.memset(v_ext[:, :, HD:HD + 1], 1.0).then_inc(s_consts, 1)

            dve.wait_ge(s_act_setup, 1)
            for k in range(XK):
                nc.vector.scalar_tensor_tensor(
                    wq_l[:, k].rearrange("p (two a) -> p two a", two=2),
                    wq_raw[:, k * DIM:(k + 1) * DIM].rearrange("p (a two) -> p two a", two=2), 0.25,
                    wq_h[:, k].bitcast(f32).rearrange("p (two a) -> p two a", two=2), ALU.mult, ALU.subtract)
            for k in range(CK):
                raw = wkv_raw[:, k * 1024:(k + 1) * 1024]
                nc.vector.tensor_tensor(wkv_l[:, k, 0:DIM].rearrange("p (two a) -> p two a", two=2),
                                        raw[:, 0:DIM].rearrange("p (a two) -> p two a", two=2),
                                        wkv_h[:, k, 0:DIM].bitcast(f32).rearrange("p (two a) -> p two a", two=2),
                                        ALU.subtract)
                nc.vector.tensor_tensor(wkv_l[:, k, DIM:1024], raw[:, DIM:1024],
                                        wkv_h[:, k, DIM:1024].bitcast(f32), ALU.subtract)
            nc.vector.tensor_tensor(wout_l[:].rearrange("p k n -> p (k n)"), wout_raw,
                                    wout_h[:].rearrange("p k n -> p (k n)").bitcast(f32),
                                    ALU.subtract).then_inc(s_split, 1)
            for k, bank in enumerate((score_a, score_b, dense, gene)):
                dve.wait_ge(s_wcT_h, k + 1)
                nc.vector.scalar_tensor_tensor(wcT_l[:, k], bank[:], wc_scale[:, k:k + 1],
                                               wcT_h[:, k].bitcast(f32), ALU.mult,
                                               ALU.subtract).then_inc(s_split_wcT, 1)
            dve.wait_ge(s_act_setup, 2)
            nc.vector.tensor_tensor(wduT_l[:], score_a[0:GD, :], wduT_h[0:GD].bitcast(f32),
                                    ALU.subtract).then_inc(s_split_duT, 1)

            def norm1(t):
                hold(dve)
                dve.wait_ge(s_x, (t + 1) * 16)
                nc.vector.bn_stats(bn1[:], slot(t)).then_inc(s_bn1, 1)
                hold(dve)
                dve.wait_ge(s_bn1, t + 1)
                nc.vector.bn_aggr(mv1[:], bn1[:]).then_inc(s_mv1, 1)
                dve.wait_ge(s_mv1, t + 1)
                nc.vector.tensor_scalar(var1[:], mv1[:, 1:2], LN_EPS, None, ALU.add).then_inc(s_var1, 1)
                dve.wait_ge(s_rstd1, t + 1)
                if not first(t):
                    dve.wait_ge(s_xT, t)
                nc.vector.tensor_scalar(xn[:], slot(t), mv1[:, 0:1], rstd1[:], ALU.subtract,
                                        ALU.mult).then_inc(s_xn, 1)

            def x_lo(t):
                dve.wait_ge(s_xT_h, t + 1)
                nc.vector.tensor_tensor(xT_l[:], dense[:, 0:DIM], xT_h[:].bitcast(f32),
                                        ALU.subtract).then_inc(s_xT_l, 1)
                dve.wait_ge(s_cT_h, t + 1)
                nc.vector.tensor_tensor(cT_l[:], dense[:, 512:512 + CTX], cT_h[:].bitcast(f32),
                                        ALU.subtract).then_inc(s_cT_l, 1)

            def group_max(t, g):
                dve.wait_ge(s_sc[g], t + 1)
                if g == 0 and not first(t):
                    dve.wait_ge(s_nml, t)
                nc.vector.tensor_reduce(row_max[:, g * GH:(g + 1) * GH],
                                        score_of[g][:].rearrange("p (s k) -> p s k", k=P),
                                        mybir.AxisListType.X, ALU.max).then_inc(s_mx[g], 1)

            def negate_max(t):
                both = neg_max[:].rearrange("p (r l s) -> p r l s", r=2, l=2)
                maxima = row_max[:].unsqueeze(1).broadcast_to([P, 2, HEADS])
                for g in range(GROUPS):
                    dve.wait_ge(s_mx[g], t + 1)
                if not first(t):
                    dve.wait_ge(s_nmT, t)
                nc.vector.tensor_scalar(both[:, :, 0], maxima, -1.0, None, ALU.mult).then_inc(s_nmh, 1)
                dve.wait_ge(s_nmh, t + 1)
                nc.vector.scalar_tensor_tensor(both[:, :, 1], maxima, -1.0, both[:, :, 0], ALU.mult,
                                               ALU.subtract).then_inc(s_nml, 1)

            def normalise(t):
                o = score_b[:].rearrange("p (h e) -> p h e", e=32)
                dve.wait_ge(s_o, t + 1)
                nc.vector.reciprocal(inv_sum[:].unsqueeze(2), o[:, :, HD:HD + 1]).then_inc(s_inv, 1)
                dve.wait_ge(s_inv, t + 1)
                if not first(t):
                    dve.wait_ge(s_aT, t)
                nc.vector.tensor_tensor(attn[:].rearrange("p (h d) -> p h d", d=HD), o[:, :, 0:HD],
                                        inv_sum[:].unsqueeze(2).broadcast_to([P, HEADS, HD]),
                                        ALU.mult).then_inc(s_attn, 1)

            def attn_lo(t):
                dve.wait_ge(s_aT_h, t + 1)
                nc.vector.tensor_tensor(aT_l[:], score_a[:, 0:DIM], aT_h[:].bitcast(f32),
                                        ALU.subtract).then_inc(s_aT_l, 1)

            def residual(t):
                dve.wait_ge(s_proj, t + 1)
                dve.wait_ge(s_xb, t + 1)
                nc.vector.tensor_tensor(slot(t), score_a[:, 512:1024], slot(t), ALU.add).then_inc(s_x1, 1)

            def norm2_stats(t):
                hold(dve)
                dve.wait_ge(s_x1, t + 1)
                nc.vector.bn_stats(bn2[:], slot(t)).then_inc(s_bn2, 1)
                hold(dve)
                dve.wait_ge(s_bn2, t + 1)
                nc.vector.bn_aggr(mv2[:], bn2[:]).then_inc(s_mv2, 1)
                dve.wait_ge(s_mv2, t + 1)
                nc.vector.tensor_scalar(var2[:], mv2[:, 1:2], 1.0 + RMS_EPS, RMS_EPS * LN_EPS, ALU.mult,
                                        ALU.add).then_inc(s_var2, 1)

            def norm2_apply(t):
                dve.wait_ge(s_norm2, t + 1)
                if not first(t):
                    dve.wait_ge(s_yT, t)
                nc.vector.tensor_scalar(yn[:], slot(t), mv2[:, 0:1], rstd2[:], ALU.subtract,
                                        ALU.mult).then_inc(s_yn, 1)

            def y_lo(t):
                dve.wait_ge(s_yT_h, t + 1)
                nc.vector.tensor_tensor(yT_l[:], score_a[:, 0:DIM], yT_h[:].bitcast(f32),
                                        ALU.subtract).then_inc(s_yT_l, 1)

            def keep_norm(t):
                dve.wait_ge(s_norm2, t + 1)
                if not first(t):
                    dve.wait_ge(s_t2, t)
                nc.vector.tensor_copy(normx[:, 0:1], mv2[:, 0:1])
                nc.vector.tensor_copy(normx[:, 1:2], rstd2[:]).then_inc(s_normx, 1)

            def find_top(t, n):
                hold(dve)
                if n == 0:
                    dve.wait_ge(s_lgr[0], t + 1)
                    dve.wait_ge(s_lgr[1], t + 1)
                    if not first(t):
                        dve.wait_ge(s_rem[3], t)
                else:
                    dve.wait_ge(s_rem[n - 1], t + 1)
                nc.vector.max(top[:, 8 * n:8 * n + 8], logit if n == 0 else rest).then_inc(s_top[n], 1)

            def remove_top(t, n):
                hold(dve)
                dve.wait_ge(s_top[n], t + 1)
                if n == 0 and not first(t):
                    dve.wait_ge(s_gw, t)
                nc.vector.match_replace(rest, top[:, 8 * n:8 * n + 8], logit if n == 0 else rest,
                                        REMOVED).then_inc(s_rem[n], 1)

            def negate_top(t):
                dve.wait_ge(s_top[0], t + 1)
                if not first(t):
                    dve.wait_ge(s_gexp, t)
                nc.vector.tensor_scalar(neg_top[:], top[:, 0:1], -1.0, None, ALU.mult).then_inc(s_ntop, 1)

            def mask(t):
                dve.wait_ge(s_rem[3], t + 1)
                dve.wait_ge(s_gexp, t + 1)
                nc.vector.scalar_tensor_tensor(gene_w, rest, REMOVED, gene_w, ALU.is_equal, ALU.mult,
                                               accum_out=gene_sum[:]).then_inc(s_gw, 1)
                dve.wait_ge(s_gw, t + 1)
                nc.vector.reciprocal(inv_gene_sum[:], gene_sum[:]).then_inc(s_ginv, 1)

            def scale_e(t):
                dve.wait_ge(s_e, t + 1)
                dve.wait_ge(s_ginv, t + 1)
                if not first(t):
                    dve.wait_ge(s_eT, t)
                nc.vector.tensor_scalar(e_sb[:], gene[:, 0:GD].unsqueeze(1).broadcast_to([P, 2, GD]),
                                        inv_gene_sum[:], None, ALU.mult).then_inc(s_e_sb, 1)

            def e_lo(t):
                dve.wait_ge(s_eT_h, t + 1)
                if not first(t):
                    dve.wait_ge(s_upp, t)
                nc.vector.tensor_copy(eT_hl[0:GD], eT_h[0:GD].bitcast(f32))
                nc.vector.tensor_tensor(eT_hl[GD:2 * GD], gene[GD:2 * GD, 512:512 + P],
                                        eT_h[GD:2 * GD].bitcast(f32), ALU.subtract).then_inc(s_eT_l, 1)

            def combine(t):
                dve.wait_ge(s_tanh, t + 1)
                dve.wait_ge(s_normx, t + 1)
                nc.vector.scalar_tensor_tensor(down[:], slot(t), normx[:, 0:1], down[:], ALU.subtract,
                                               ALU.mult).then_inc(s_t1, 1)
                dve.wait_ge(s_t1, t + 1)
                dve.wait_ge(s_upp, t + 1)
                nc.vector.scalar_tensor_tensor(down[:], down[:], normx[:, 1:2], gene[:, 512:1024], ALU.mult,
                                               ALU.mult).then_inc(s_t2, 1)

            def iteration(a, b, c):
                if c is not None:
                    keep_norm(c)
                if a is not None:
                    norm1(a)
                if b is not None:
                    group_max(b, 0)
                    group_max(b, 1)
                if a is not None:
                    x_lo(a)
                if b is not None:
                    group_max(b, 2)
                    group_max(b, 3)
                    negate_max(b)
                if c is not None:
                    find_top(c, 0)
                    negate_top(c)
                    remove_top(c, 0)
                    find_top(c, 1)
                    remove_top(c, 1)
                    find_top(c, 2)
                    remove_top(c, 2)
                if b is not None:
                    normalise(b)
                if c is not None:
                    find_top(c, 3)
                if b is not None:
                    attn_lo(b)
                if c is not None:
                    remove_top(c, 3)
                    mask(c)
                if b is not None:
                    residual(b)
                    norm2_stats(b)
                if c is not None:
                    scale_e(c)
                if b is not None:
                    norm2_apply(b)
                if c is not None:
                    e_lo(c)
                if b is not None:
                    y_lo(b)
                if c is not None:
                    combine(c)

            run(dve, iteration)

        @block.tensor
        def _(pe):
            pe.wait_ge(s_ident, 1)
            pe.wait_ge(s_wc, 16)
            for k, bank in enumerate((score_a, score_b, dense, gene)):
                for g in range(GK):
                    last = nc.tensor.transpose(bank[:, g * P:(g + 1) * P], wc_raw[:, g, k * P:(k + 1) * P], ident[:])
                last.then_inc(s_wcT, 1)
            pe.wait_ge(s_up, 1)
            pe.wait_ge(s_split_wcT, 1)
            for n in range(2):
                for k in range(XK):
                    last = nc.tensor.transpose(score_a[:, n * DIM + k * P:n * DIM + (k + 1) * P],
                                               du_raw[:, n, k], ident[:])
            last.then_inc(s_duT, 1)
            pe.wait_ge(s_consts, 1)
            pe.wait_ge(s_split, 1)
            pe.wait_ge(s_split_wcT, 4)
            pe.wait_ge(s_split_duT, 1)

            def three_pass(out, xs, ws, chunks):
                (xh, xl), (wh, wl) = xs, ws
                n, steps = 0, 3 * chunks
                for k in range(chunks):
                    for lhs, rhs in ((xh, wh), (xh, wl), (xl, wh)):
                        last = nc.tensor.matmul(out, lhs[:, k * P:(k + 1) * P], rhs(k), start=(n == 0),
                                                stop=(n == steps - 1))
                        n += 1
                return last

            def columns(w, at):
                return lambda k: w[:, k, at:at + 512]

            def transpose_x(t):
                pe.wait_ge(s_xn, t + 1)
                if not first(t):
                    pe.wait_ge(s_trr[2], t)
                for k in range(XK):
                    last = nc.tensor.transpose(dense[:, k * P:(k + 1) * P], xn[:, k * P:(k + 1) * P], ident[:])
                last.then_inc(s_xT, 1)
                pe.wait_ge(s_ctx, (t + 1) * 16)
                if not first(t):
                    pe.wait_ge(s_trr[3], t)
                for k in range(CK):
                    last = nc.tensor.transpose(dense[:, 512 + k * P:512 + (k + 1) * P],
                                               ctx_sb[:, k * P:(k + 1) * P], ident[:])
                last.then_inc(s_cT, 1)

            def project_q(t):
                pe.wait_ge(s_xT_h, t + 1)
                pe.wait_ge(s_xT_l, t + 1)
                three_pass(dense[:, 0:512], (xT_h, xT_l), (columns(wq_h, 0), columns(wq_l, 0)),
                           XK).then_inc(s_q, 1)

            def project_k(t):
                pe.wait_ge(s_cT_h, t + 1)
                pe.wait_ge(s_cT_l, t + 1)
                three_pass(dense[:, 512:1024], (cT_h, cT_l), (columns(wkv_h, 0), columns(wkv_l, 0)),
                           CK).then_inc(s_k, 1)

            def project_v(t):
                pe.wait_ge(s_q_sb, t + 1)
                if not first(t):
                    pe.wait_ge(s_oT[0], t)
                three_pass(dense[:, 0:512], (cT_h, cT_l), (columns(wkv_h, 512), columns(wkv_l, 512)),
                           CK).then_inc(s_v, 1)

            def transpose_qk(t, n):
                if n == 0:
                    pe.wait_ge(s_hi, t + 1)
                    pe.wait_ge(s_lo, t + 1)
                    pe.wait_ge(s_v_sb, t + 1)
                elif n == 1:
                    pe.wait_ge(s_k_sb, t + 1)
                    if not first(t):
                        pe.wait_ge(s_oT[1], t)
                else:
                    pe.wait_ge(s_trr[n - 2], t + 1)
                half = dense[:, (n % 2) * 512:(n % 2 + 1) * 512].bitcast(f16)
                for m in range(8):
                    last = nc.tensor.transpose(half[:, m * P:(m + 1) * P],
                                               pair_in(n // 2, (n % 2) * 8 + m), ident16[:])
                last.then_inc(s_tr[n], 1)

            def scores(t, g):
                if g == 0:
                    for n in range(4):
                        pe.wait_ge(s_trr[n], t + 1)
                    if not first(t):
                        pe.wait_ge(s_x1, t)
                        pe.wait_ge(s_yT_l, t)
                elif g == 1:
                    if not first(t):
                        pe.wait_ge(s_attn, t)
                else:
                    pe.wait_ge(s_mx[g - 2], t + 1)
                for r in range(GH):
                    head = g * GH + r
                    at = (r % 2) * 512 + (r // 2) * P
                    last = nc.tensor.matmul(score_of[g][:, at:at + P], rows_of(qT, head), rows_of(kT, head),
                                            start=True, stop=True)
                last.then_inc(s_sc[g], 1)

            def transpose_neg_max(t):
                pe.wait_ge(s_nmh, t + 1)
                pe.wait_ge(s_nml, t + 1)
                nc.tensor.transpose(score_a[:, 0:64].bitcast(bf16), neg_max[:], identb[:]).then_inc(s_nmT, 1)

            def scoresT(t, g):
                if g == 0:
                    pe.wait_ge(s_mx[3], t + 1)
                elif g == 1:
                    pe.wait_ge(s_nmT_sb, t + 1)
                else:
                    pe.wait_ge(s_ex[g - 2], t + 1)
                if g == 0:
                    pe.wait_ge(s_nmT_sb, t + 1)
                for r in range(0, GH, 2):
                    for step in range(2):
                        for odd in range(2):
                            head = g * GH + r + odd
                            at = odd * 512 + (r // 2) * P
                            out = scoreT_of[g][:, at:at + P]
                            if step == 0:
                                nc.tensor.matmul(out, rows_of(kT, head), rows_of(qT, head), start=True, stop=False)
                            else:
                                rows = slice(64 * odd, 64 * odd + 64)
                                place = g * GH + odd * 4 + r // 2
                                last = nc.tensor.matmul(out, select[rows, place], neg_maxT[rows, :],
                                                        start=False, stop=True)
                last.then_inc(s_st[g], 1)

            def values(t, g):
                if g == 0:
                    pe.wait_ge(s_v_sb, t + 1)
                pe.wait_ge(s_ex[g], t + 1)
                for r in range(GH):
                    head = g * GH + r
                    rows = slice(32 * (r % 4), 32 * (r % 4) + 32)
                    at = (2 * g + r // 4) * P
                    slot_at = ((r % 2) * 4 + r // 2) * P
                    last = nc.tensor.matmul(dense[rows, at:at + P], v_ext[:, head], probs[g % 2][:, slot_at:slot_at + P],
                                            start=True, stop=True)
                last.then_inc(s_av[g], 1)

            def transpose_o(t):
                pe.wait_ge(s_oT[0], t + 1)
                pe.wait_ge(s_oT[1], t + 1)
                pe.wait_ge(s_ex[2], t + 1)
                for n in range(8):
                    last = nc.tensor.transpose(score_b[:, n * P:(n + 1) * P], oT_sb[:, n * P:(n + 1) * P], ident[:])
                last.then_inc(s_o, 1)

            def transpose_attn(t):
                pe.wait_ge(s_attn, t + 1)
                pe.wait_ge(s_ex[3], t + 1)
                for k in range(XK):
                    last = nc.tensor.transpose(score_a[:, k * P:(k + 1) * P], attn[:, k * P:(k + 1) * P], ident[:])
                last.then_inc(s_aT, 1)

            def project_out(t):
                pe.wait_ge(s_aT_h, t + 1)
                pe.wait_ge(s_aT_l, t + 1)
                three_pass(score_a[:, 512:1024], (aT_h, aT_l), (columns(wout_h, 0), columns(wout_l, 0)),
                           XK).then_inc(s_proj, 1)

            def transpose_y(t):
                pe.wait_ge(s_yn, t + 1)
                pe.wait_ge(s_aT_l, t + 1)
                for k in range(XK):
                    last = nc.tensor.transpose(score_a[:, k * P:(k + 1) * P], yn[:, k * P:(k + 1) * P], ident[:])
                last.then_inc(s_yT, 1)

            def logits(t, n):
                if n == 0:
                    pe.wait_ge(s_yT_h, t + 1)
                    pe.wait_ge(s_yT_l, t + 1)
                    if not first(t):
                        pe.wait_ge(s_tanh, t)
                elif not first(t):
                    pe.wait_ge(s_t2, t)
                three_pass(gene[:, n * 512:(n + 1) * 512], (yT_h, yT_l),
                           (columns(wcT_h, n * 512), columns(wcT_l, n * 512)), XK).then_inc(s_lg[n], 1)

            def transpose_w(t, n):
                pe.wait_ge(s_gw, t + 1)
                pe.wait_ge(s_lgr[n], t + 1)
                for g in range(4 * n, 4 * n + 4):
                    last = nc.tensor.transpose(gene[:, g * P:(g + 1) * P], gene_w[:, g * P:(g + 1) * P], ident[:])
                last.then_inc(s_wT[n], 1)

            def express(t):
                pe.wait_ge(s_wTr[0], t + 1)
                pe.wait_ge(s_wTr[1], t + 1)
                for g in range(GK):
                    last = nc.tensor.matmul(gene[:, 0:GD], gene_wT[:, g * P:(g + 1) * P], genes_sb[:, g],
                                            start=(g == 0), stop=(g == GK - 1))
                last.then_inc(s_e, 1)

            def transpose_e(t):
                pe.wait_ge(s_e_sb, t + 1)
                nc.tensor.transpose(gene[:, 512:512 + P], e_sb[:].rearrange("p r c -> p (r c)"), ident[:]).then_inc(s_eT, 1)

            def down_up(t):
                pe.wait_ge(s_eT_h, t + 1)
                pe.wait_ge(s_eT_l, t + 1)
                for n, done in enumerate((s_dn, s_upp)):
                    cols = slice(n * DIM, (n + 1) * DIM)
                    nc.tensor.matmul(gene[:, cols], eT_hl[:], wduT_h[:, cols], start=True, stop=False)
                    nc.tensor.matmul(gene[:, cols], eT_h[0:GD], wduT_l[:, cols], start=False,
                                     stop=True).then_inc(done, 1)

            def iteration(a, b, c):
                if b is not None:
                    scores(b, 0)
                    scores(b, 1)
                if c is not None:
                    logits(c, 0)
                if a is not None:
                    transpose_x(a)
                if b is not None:
                    scores(b, 2)
                if c is not None:
                    logits(c, 1)
                if b is not None:
                    scores(b, 3)
                if a is not None:
                    project_q(a)
                if b is not None:
                    transpose_neg_max(b)
                if a is not None:
                    project_k(a)
                if b is not None:
                    if a is not None:
                        pe.wait_ge(s_q_sb, a + 1)
                        pe.wait_ge(s_k_sb, a + 1)
                    scoresT(b, 0)
                    scoresT(b, 1)
                    for g in range(GROUPS):
                        values(b, g)
                        if g + 2 < GROUPS:
                            scoresT(b, g + 2)
                if a is not None:
                    project_v(a)
                if b is not None:
                    transpose_o(b)
                    transpose_attn(b)
                    project_out(b)
                if c is not None:
                    transpose_w(c, 0)
                    transpose_w(c, 1)
                    express(c)
                    transpose_e(c)
                    down_up(c)
                if b is not None:
                    transpose_y(b)
                if a is not None:
                    for n in range(4):
                        transpose_qk(a, n)

            run(pe, iteration)


NAMES = ['x', 'ctx_1024', 'fside_BxSx2_0', 'L0_xattn_Wq', 'L0_xattn_Wkv', 'L0_xattn_Wout', 'L0_xattn_bout',
         'L0_ffn_Wc', 'L0_ffn_temperature', 'L0_ffn_genes', 'L0_ffn_Wd', 'L0_ffn_Wu', 'L0_ffn_norm_w',
         'L0_ffn_scale']


def kernel(**inputs):
    import numpy as np
    import concourse.bacc as bacc
    from concourse.bass_utils import run_bass_kernel_spmd

    nc = bacc.Bacc("TRN2", target_bir_lowering=False, num_devices=1)
    arrays, args = {}, []
    for name in NAMES:
        a = np.ascontiguousarray(inputs[name])
        a = a.reshape(a.shape or (1,))
        if name == 'L0_ffn_norm_w':
            a = np.ascontiguousarray(a.reshape(XK, P).T)
        arrays[name + "_dram"] = a
        args.append(nc.dram_tensor(name + "_dram", a.shape, mybir.dt.from_np(a.dtype), kind="ExternalInput").ap())
    out = nc.dram_tensor("out_dram", (TILES, P, DIM), f32, kind="ExternalOutput").ap()
    build(nc, *args, out)
    result = run_bass_kernel_spmd(nc, [arrays], core_ids=[0])
    return result.results[0]["out_dram"]
```

```python
from contextlib import ExitStack

import concourse.bass as bass
from concourse import mybir

P = 128
TILES = 16
DIM, CTX = 512, 256
HEADS, HD = 32, 16
GENES, GD = 1024, 64
TOP = 32
XK, CK, GK = DIM // P, CTX // P, GENES // P
XSLOTS = 6
GROUPS = 4
GH = HEADS // GROUPS
LN_EPS = 1e-5
RMS_EPS = 2.0 ** -23
REMOVED = -3.0e38
ROPE_FREQS = [10000.0 ** (-j / 4) for j in range(4)]
TWO_PI_HI, TWO_PI_LO = 6.28125, 6.283185307179586 - 6.28125

f32, f32r = mybir.dt.float32, mybir.dt.float32r
f16, bf16, i32 = mybir.dt.float16, mybir.dt.bfloat16, mybir.dt.int32
ALU = mybir.AluOpType
ACT = mybir.ActivationFunctionType


def build(nc, x, ctx, pos, wq, wkv, wout, bout, wc, temp, genes, wd, wu, norm_w, scale, out):
    stack = ExitStack()
    with stack:
        def sb(name, shape, dt=f32):
            return stack.enter_context(nc.sbuf_tensor(name, shape, dt))

        def ps(name):
            return stack.enter_context(nc.psum_tensor(name, [P, 1024], f32))

        def sem(name):
            return stack.enter_context(nc.semaphore(name))

        wq_h, wq_l = sb("wq_h", [P, XK, DIM], f32r), sb("wq_l", [P, XK, DIM], f32r)
        wkv_h, wkv_l = sb("wkv_h", [P, CK, 2 * DIM], f32r), sb("wkv_l", [P, CK, 2 * DIM], f32r)
        wout_h, wout_l = sb("wout_h", [P, XK, DIM], f32r), sb("wout_l", [P, XK, DIM], f32r)
        wcT_h, wcT_l = sb("wcT_h", [P, XK, GENES], f32r), sb("wcT_l", [P, XK, GENES], f32r)
        wduT_h, wduT_l = sb("wduT_h", [2 * GD, 2 * DIM], f32r), sb("wduT_l", [GD, 2 * DIM], f32r)
        genes_sb = sb("genes_sb", [P, GK, GD])
        bout_sb = sb("bout_sb", [P, DIM])
        norm_sb = sb("norm_sb", [P, XK])
        wc_scale = sb("wc_scale", [P, XK])
        up_scale = sb("up_scale", [P, XK])
        knob = sb("knob", [P, 4])
        minus_half = sb("minus_half", [P, 1])
        ident = sb("ident", [P, P])
        ident16 = sb("ident16", [P, P], f16)
        identb = sb("identb", [P, P], bf16)
        pick = sb("pick", [P, HEADS])
        select = sb("select", [P, HEADS, P], bf16)
        pos_sb = sb("pos_sb", [P, TILES, 2])
        cos_t, sin_t = sb("cos_t", [P, TILES * 8]), sb("sin_t", [P, TILES * 8])

        stage_a = sb("stage_a", [P, 4096])
        stage_b = sb("stage_b", [P, 6144])
        wc_raw = stage_a[:, :].rearrange("p (g d) -> p g d", d=DIM)
        wq_raw = stage_b[:, 0:2048]
        wkv_raw = stage_b[:, 2048:4096]
        wout_raw = stage_b[:, 4096:6144]
        probs = [stage_a[:, 0:1024], stage_a[:, 1024:2048]]
        gene_w = stage_a[:, 2048:3072]
        gene_wT = stage_a[:, 3072:4096]
        qk_sb = stage_b[:, 0:1024]
        qk_cos, qk_sin = stage_b[:, 1024:2048], stage_b[:, 2048:3072]
        logit = stage_b[:, 3072:4096]
        rest = stage_b[:, 4096:5120]
        oT_sb = stage_b[:, 5120:6144]

        x_ring = sb("x_ring", [P, XSLOTS * DIM])
        ctx_sb = sb("ctx_sb", [P, CTX])
        xn = sb("xn", [P, DIM])
        xT_h, xT_l = sb("xT_h", [P, DIM], f32r), sb("xT_l", [P, DIM], f32r)
        cT_h, cT_l = sb("cT_h", [P, CTX], f32r), sb("cT_l", [P, CTX], f32r)
        turned = sb("turned", [P, 2 * DIM])
        parts = sb("parts", [P, 2 * HEADS, 4, HD], f16)
        qT, kT = sb("qT", [P, HEADS // 2 * P], f16), sb("kT", [P, HEADS // 2 * P], f16)
        v_ext = sb("v_ext", [P, HEADS, 32])
        attn = sb("attn", [P, DIM])
        aT_h, aT_l = sb("aT_h", [P, DIM], f32r), sb("aT_l", [P, DIM], f32r)
        yn = sb("yn", [P, DIM])
        du_raw = turned[:].rearrange("p (n k c) -> p n k c", n=2, k=XK)
        angle = attn[:, 0:3 * TILES * 8].rearrange("p (n a) -> p n a", n=3)
        turns = yn[:, 0:TILES * 8].bitcast(i32)
        yT_h, yT_l = sb("yT_h", [P, DIM], f32r), sb("yT_l", [P, DIM], f32r)
        down = sb("down", [P, DIM])
        row_max = sb("row_max", [P, HEADS])
        neg_max = sb("neg_max", [P, 4 * HEADS], bf16)
        neg_maxT = sb("neg_maxT", [P, P], bf16)
        inv_sum = sb("inv_sum", [P, HEADS])
        bn1, bn2 = sb("bn1", [P, 6]), sb("bn2", [P, 6])
        mv1, mv2 = sb("mv1", [P, 2]), sb("mv2", [P, 2])
        var1, rstd1 = sb("var1", [P, 1]), sb("rstd1", [P, 1])
        var2, rstd2 = sb("var2", [P, 1]), sb("rstd2", [P, 1])
        normx = sb("normx", [P, 2])
        top = sb("top", [P, TOP])
        neg_top = sb("neg_top", [P, 1])
        gene_sum, inv_gene_sum = sb("gene_sum", [P, 1]), sb("inv_gene_sum", [P, 1])
        e_sb = sb("e_sb", [P, 2, GD])
        eT_h = sb("eT_h", [2 * GD, P], f32r)
        eT_hl = sb("eT_hl", [2 * GD, P], f32r)

        score_a, score_b, dense, gene = ps("score_a"), ps("score_b"), ps("dense"), ps("gene")

        s_wq, s_wkv, s_wout, s_wc, s_du, s_small = (sem(n) for n in (
            "wq_in", "wkv_in", "wout_in", "wc_in", "du_in", "small_in"))
        s_ident = sem("ident_ready")
        s_pool_setup = sem("pool_setup")
        s_setup = sem("dve_setup")
        s_act_setup = sem("act_setup")
        s_wcT = sem("wcT_in_psum")
        s_duT = sem("duT_in_psum")
        s_trig = sem("trig_ready")
        s_angle, s_scales, s_consts, s_up = (sem(n) for n in (
            "angles_ready", "scales_ready", "constants_ready", "up_weights_scaled"))
        s_split, s_split_wcT, s_split_duT = sem("weights_split"), sem("wcT_split"), sem("duT_split")
        s_wcT_h = sem("wcT_h_done")
        s_x, s_ctx = sem("x_loaded"), sem("ctx_loaded")
        s_bn1, s_mv1, s_var1, s_rstd1, s_xn = (sem(n) for n in (
            "bn1_done", "mv1_done", "var1_done", "rstd1_done", "xn_done"))
        s_xT, s_cT = sem("xT_in_psum"), sem("cT_in_psum")
        s_xT_h, s_xT_l, s_cT_h, s_cT_l = (sem(n) for n in ("xT_h_done", "xT_l_done", "cT_h_done", "cT_l_done"))
        s_q, s_k, s_v = sem("q_in_psum"), sem("k_in_psum"), sem("v_in_psum")
        s_q_sb, s_k_sb, s_v_sb = sem("q_read"), sem("k_read"), sem("v_read")
        s_cosm, s_sinm, s_rot, s_hi, s_lo = ([sem(f"{x}_{what}") for x in "qk"] for what in (
            "cos_done", "sin_done", "rope_done", "hi_done", "lo_done"))
        s_xb = sem("bout_added")
        s_tr = [sem(f"qkT{n}_in_psum") for n in range(4)]
        s_trr = [sem(f"qkT{n}_read") for n in range(4)]
        s_sc = [sem(f"scores{g}_in_psum") for g in range(GROUPS)]
        s_mx = [sem(f"max{g}_done") for g in range(GROUPS)]
        s_nmh, s_nml = sem("neg_max_hi_done"), sem("neg_max_lo_done")
        s_nmT, s_nmT_sb = sem("neg_maxT_in_psum"), sem("neg_maxT_read")
        s_st = [sem(f"scoresT{g}_in_psum") for g in range(GROUPS)]
        s_ex = [sem(f"exp{g}_done") for g in range(GROUPS)]
        s_av = [sem(f"values{g}_done") for g in range(GROUPS)]
        s_oT = [sem(f"oT{n}_read") for n in range(2)]
        s_o, s_inv, s_attn = sem("o_in_psum"), sem("inv_sum_done"), sem("attn_done")
        s_aT, s_aT_h, s_aT_l = sem("attnT_in_psum"), sem("attnT_h_done"), sem("attnT_l_done")
        s_proj, s_x1 = sem("proj_in_psum"), sem("x1_done")
        s_bn2, s_mv2, s_var2, s_norm2, s_yn = (sem(n) for n in (
            "bn2_done", "mv2_done", "var2_done", "norm2_done", "yn_done"))
        s_mean2 = sem("mean2_copied")
        s_yT, s_yT_h, s_yT_l = sem("ynT_in_psum"), sem("ynT_h_done"), sem("ynT_l_done")
        s_normx = sem("norm_copied")
        s_lg = [sem(f"logits{n}_in_psum") for n in range(2)]
        s_lgr = [sem(f"logits{n}_read") for n in range(2)]
        s_top = [sem(f"top{n}_found") for n in range(4)]
        s_rem = [sem(f"top{n}_removed") for n in range(4)]
        s_ntop, s_gexp, s_gw, s_ginv = (sem(n) for n in ("neg_top_done", "gene_exp_done", "gene_w_done", "inv_gene_sum_done"))
        s_wT = [sem(f"gene_wT{n}_in_psum") for n in range(2)]
        s_wTr = [sem(f"gene_wT{n}_read") for n in range(2)]
        s_e, s_e_sb, s_eT, s_eT_h, s_eT_l = (sem(n) for n in ("e_in_psum", "e_scaled", "eT_in_psum", "eT_h_done", "eT_l_done"))
        s_dn, s_upp, s_tanh, s_t1, s_t2, s_y = (sem(n) for n in (
            "down_in_psum", "up_in_psum", "tanh_done", "t1_done", "t2_done", "y_done"))
        s_out = sem("out_stored")

        def slot(t):
            if isinstance(t, int):
                return x_ring[:, (t % XSLOTS) * DIM:(t % XSLOTS + 1) * DIM]
            return x_ring[:, bass.ds((t % XSLOTS) * DIM, DIM)]

        def trig(table, t):
            at = table[:, t * 8:(t + 1) * 8] if isinstance(t, int) else table[:, bass.ds(t * 8, 8)]
            return at.unsqueeze(1).broadcast_to([P, 2 * HEADS, 8])

        q_parts, k_parts = parts[:, 0:HEADS], parts[:, HEADS:2 * HEADS]

        def head_major(t, n):
            return t[:, n * DIM:(n + 1) * DIM].rearrange("p (h d) -> p h d", d=HD)

        def pair_in(n, m):
            at = n * HEADS + 2 * m
            return parts[:, at:at + 2].rearrange("p h l d -> p (h l d)")

        def rows_of(t, head):
            r = 64 * (head % 2)
            return t[r:r + 64, (head // 2) * P:(head // 2 + 1) * P]

        score_of = [score_a, score_b, score_a, score_b]
        scoreT_of = [score_b, score_a, score_b, score_a]

        block = stack.enter_context(nc.Block())

        def last_tile(t):
            return isinstance(t, int) and t == TILES - 1

        def first(t):
            return isinstance(t, int) and t == 0

        def hold(eng):
            eng.wait_ge(s_trig, 1)

        def run(eng, iteration):
            for i in range(5):
                iteration(*(i - n if i >= n else None for n in range(5)))
            with eng.Fori(5, TILES) as i:
                iteration(i, i - 1, i - 2, i - 3, i - 4)
            for i in range(TILES, TILES + 4):
                iteration(*(i - n if i - n < TILES else None for n in range(5)))

        @block.sync
        def _(sp):
            sp.dma_start(wc_raw, wc.rearrange("(g p) d -> p g d", p=P)).then_inc(s_wc, 16)
            for n, w in enumerate((wd, wu)):
                for half in range(2):
                    sp.dma_start(du_raw[:, n, :, half * GD:(half + 1) * GD],
                                 w.rearrange("(k p) c -> p k c", p=P)).then_inc(s_du, 16)

            def load_x(t):
                if isinstance(t, int):
                    src = x[t]
                else:
                    src = x[bass.ds(t, 1)].rearrange("o p n -> p (o n)")
                sp.dma_start(slot(t), src).then_inc(s_x, 16)

            def load_ctx(t):
                if isinstance(t, int):
                    src = ctx[t]
                else:
                    src = ctx[bass.ds(t, 1)].rearrange("o p n -> p (o n)")
                sp.dma_start(ctx_sb[:], src).then_inc(s_ctx, 16)

            def store(t):
                if isinstance(t, int):
                    dst = out[t]
                else:
                    dst = out[bass.ds(t, 1)].rearrange("o p n -> p (o n)")
                sp.dma_start(dst, slot(t)).then_inc(s_out, 16)

            load_x(0)
            load_ctx(0)

            def next_x(t):
                sp.wait_ge(s_x, (t + 1) * 16)
                if not isinstance(t, int) or t >= XSLOTS:
                    sp.wait_ge(s_out, (t + 2 - XSLOTS) * 16)
                load_x(t + 1)

            def next_ctx(t):
                sp.wait_ge(s_cT, t + 1)
                load_ctx(t + 1)

            def iteration(l, a, b, c, d):
                if l is not None and not (isinstance(l, int) and l == TILES - 1):
                    next_x(l)
                if a is not None and not (isinstance(a, int) and a == TILES - 1):
                    next_ctx(a)
                if d is not None:
                    sp.wait_ge(s_y, d + 1)
                    store(d)

            for i in range(XSLOTS):
                iteration(*(i - n if i >= n else None for n in range(5)))
            with sp.Fori(XSLOTS, TILES - 1) as i:
                iteration(i, i - 1, i - 2, i - 3, i - 4)
            for i in range(TILES - 1, TILES + 4):
                iteration(*(i - n if i - n < TILES else None for n in range(5)))
            sp.wait_ge(s_out, TILES * 16)

        @block.gpsimd
        def _(pool):
            pool.memset(ident[:], 0.0).then_inc(s_pool_setup, 1)
            pool.wait_ge(s_pool_setup, 1)
            pool.affine_select(out=ident[:], in_=ident[:], compare_op=ALU.not_equal, fill=1.0, base=0,
                               pattern=[[-1, P]], channel_multiplier=1).then_inc(s_ident, 1)
            pool.memset(minus_half[:], -0.5).then_inc(s_pool_setup, 1)
            pool.wait_ge(s_pool_setup, 2)

            def ln1(t):
                pool.wait_ge(s_var1, t + 1)
                pool.tensor_tensor(rstd1[:], var1[:], minus_half[:], ALU.pow).then_inc(s_rstd1, 1)

            def add_bout(t):
                hold(pool)
                pool.wait_ge(s_xn, t + 1)
                pool.tensor_tensor(slot(t), slot(t), bout_sb[:], ALU.add).then_inc(s_xb, 1)

            def rope(t, n):
                def halves(m):
                    return m[:, n * DIM:(n + 1) * DIM].rearrange("p (a j) -> p a j", j=8)

                hold(pool)
                pool.wait_ge((s_q_sb, s_k_sb)[n], t + 1)
                if not first(t):
                    pool.wait_ge(s_rot[n], t)
                pool.tensor_tensor(halves(qk_cos), halves(qk_sb), trig(cos_t, t), ALU.mult).then_inc(s_cosm[n], 1)
                pool.tensor_tensor(halves(qk_sin), halves(qk_sb), trig(sin_t, t), ALU.mult).then_inc(s_sinm[n], 1)

            def rope_sum(t, n):
                c = qk_cos[:, n * DIM:(n + 1) * DIM].rearrange("p (two h j) -> p two h j", two=2, j=8)
                s = qk_sin[:, n * DIM:(n + 1) * DIM].rearrange("p (two h j) -> p two h j", two=2, j=8)
                o = turned[:, n * DIM:(n + 1) * DIM].rearrange("p (h two j) -> p h two j", two=2, j=8)
                pool.wait_ge(s_cosm[n], t + 1)
                pool.wait_ge(s_sinm[n], t + 1)
                if not first(t):
                    pool.wait_ge(s_hi[n], t)
                    pool.wait_ge(s_lo[n], t)
                pool.tensor_tensor(o[:, :, 0], c[:, 0], s[:, 1], ALU.subtract)
                pool.tensor_tensor(o[:, :, 1], c[:, 1], s[:, 0], ALU.add).then_inc(s_rot[n], 1)

            def split_lo(t, n):
                pool.wait_ge(s_rot[n], t + 1)
                pool.wait_ge(s_hi[n], t + 1)
                if not first(t):
                    pool.wait_ge(s_tr[2 * n + 1], t)
                to = (q_parts[:, :, 1], k_parts[:, :, 2])[n]
                pool.tensor_tensor(to, head_major(turned, n), (q_parts, k_parts)[n][:, :, 0],
                                   ALU.subtract).then_inc(s_lo[n], 1)

            def ln2(t):
                pool.wait_ge(s_var2, t + 1)
                if not first(t):
                    pool.wait_ge(s_normx, t)
                pool.tensor_tensor(rstd2[:], var2[:], minus_half[:], ALU.pow).then_inc(s_norm2, 1)

            def finish(t):
                hold(pool)
                pool.wait_ge(s_t2, t + 1)
                pool.tensor_tensor(slot(t), slot(t), down[:], ALU.add).then_inc(s_y, 1)

            pool.wait_ge(s_small, 16 * 6)
            pool.wait_ge(s_trig, 1)

            def iteration(l, a, b, c, d):
                if a is not None:
                    rope(a, 1)
                    rope(a, 0)
                if l is not None:
                    ln1(l)
                if a is not None:
                    rope_sum(a, 0)
                    rope_sum(a, 1)
                    split_lo(a, 0)
                    split_lo(a, 1)
                if b is not None:
                    ln2(b)
                if d is not None:
                    finish(d)
                if a is not None:
                    add_bout(a)

            run(pool, iteration)

        @block.scalar
        def _(act):
            act.dma_start(norm_sb[:], norm_w).then_inc(s_small, 16)
            act.dma_start(knob[:, 0:1], temp.rearrange("(o n) -> o n", o=1).broadcast_to([P, 1])).then_inc(s_small, 16)
            act.dma_start(knob[:, 1:2], scale.rearrange("(o n) -> o n", o=1).broadcast_to([P, 1])).then_inc(s_small, 16)
            act.dma_start(bout_sb[:], bout.rearrange("(o n) -> o n", o=1).broadcast_to([P, DIM])).then_inc(s_small, 16)
            act.dma_start(pos_sb[:], pos.rearrange("t p c -> p t c")).then_inc(s_small, 16)
            act.dma_start(genes_sb[:], genes.rearrange("(g p) c -> p g c", p=P)).then_inc(s_small, 16)
            act.dma_start(wq_raw, wq.rearrange("(k p) n -> p k n", p=P)).then_inc(s_wq, 16)
            act.dma_start(wkv_raw, wkv.rearrange("(k p) n -> p k n", p=P)).then_inc(s_wkv, 16)
            act.dma_start(wout_raw, wout.rearrange("(k p) n -> p k n", p=P)).then_inc(s_wout, 16)

            act.wait_ge(s_angle, 1)
            nc.scalar.activation(sin_t[:], angle[:, 0], ACT.Sin)
            nc.scalar.activation(cos_t[:], angle[:, 1], ACT.Sin).then_inc(s_trig, 1)

            act.wait_ge(s_wq, 16)
            for k in range(XK):
                nc.scalar.activation(
                    wq_h[:, k].rearrange("p (two a) -> p two a", two=2),
                    wq_raw[:, k * DIM:(k + 1) * DIM].rearrange("p (a two) -> p two a", two=2),
                    ACT.Copy, scale=0.25)
            act.wait_ge(s_wkv, 16)
            for k in range(CK):
                raw = wkv_raw[:, k * 1024:(k + 1) * 1024]
                nc.scalar.activation(wkv_h[:, k, 0:DIM].rearrange("p (two a) -> p two a", two=2),
                                     raw[:, 0:DIM].rearrange("p (a two) -> p two a", two=2), ACT.Copy)
                nc.scalar.activation(wkv_h[:, k, DIM:1024], raw[:, DIM:1024], ACT.Copy)
            act.wait_ge(s_wout, 16)
            nc.scalar.activation(wout_h[:].rearrange("p k n -> p (k n)"), wout_raw,
                                 ACT.Copy).then_inc(s_act_setup, 1)
            act.wait_ge(s_scales, 1)
            for k, bank in enumerate((score_a, score_b, dense, gene)):
                act.wait_ge(s_wcT, k + 1)
                last = nc.scalar.activation(wcT_h[:, k], bank[:], ACT.Copy, scale=wc_scale[:, k:k + 1])
                last.then_inc(s_wcT_h, 1)
            act.wait_ge(s_duT, 1)
            nc.scalar.activation(wduT_h[:], score_a[:], ACT.Copy).then_inc(s_act_setup, 1)

            def ctx_hi(t):
                act.wait_ge(s_cT, t + 1)
                if not first(t):
                    act.wait_ge(s_v, t)
                nc.scalar.activation(cT_h[:], dense[:, 512:512 + CTX], ACT.Copy).then_inc(s_cT_h, 1)

            def x_hi(t):
                act.wait_ge(s_xT, t + 1)
                if not first(t):
                    act.wait_ge(s_q, t)
                nc.scalar.activation(xT_h[:], dense[:, 0:DIM], ACT.Copy).then_inc(s_xT_h, 1)

            def read_q(t):
                act.wait_ge(s_q, t + 1)
                if not first(t):
                    act.wait_ge(s_cosm[0], t)
                    act.wait_ge(s_sinm[0], t)
                nc.scalar.activation(qk_sb[:, 0:DIM], dense[:, 0:DIM], ACT.Copy).then_inc(s_q_sb, 1)

            def read_k(t):
                act.wait_ge(s_k, t + 1)
                if not first(t):
                    act.wait_ge(s_cosm[1], t)
                    act.wait_ge(s_sinm[1], t)
                nc.scalar.activation(qk_sb[:, DIM:2 * DIM], dense[:, 512:1024], ACT.Copy).then_inc(s_k_sb, 1)

            def read_v(t):
                act.wait_ge(s_v, t + 1)
                if not first(t):
                    act.wait_ge(s_av[3], t)
                nc.scalar.activation(v_ext[:, :, 0:HD], dense[:, 0:DIM].rearrange("p (h d) -> p h d", d=HD),
                                     ACT.Copy).then_inc(s_v_sb, 1)

            def split_hi(t, n):
                act.wait_ge(s_rot[n], t + 1)
                if not first(t):
                    act.wait_ge(s_tr[2 * n + 1], t)
                to = (q_parts[:, :, 0:3:2], k_parts[:, :, 0:2])[n]
                nc.scalar.activation(to, head_major(turned, n).unsqueeze(2).broadcast_to([P, HEADS, 2, HD]),
                                     ACT.Copy).then_inc(s_hi[n], 1)

            def read_qkT(t, n):
                act.wait_ge(s_tr[n], t + 1)
                if not first(t):
                    act.wait_ge(s_st[3], t)
                dst = (qT, qT, kT, kT)[n][:, (n % 2) * 1024:(n % 2 + 1) * 1024]
                src = dense[:, (n % 2) * 512:(n % 2 + 1) * 512].bitcast(f16)
                nc.scalar.activation(dst, src, ACT.Copy).then_inc(s_trr[n], 1)

            def read_neg_max(t):
                act.wait_ge(s_nmT, t + 1)
                if not first(t):
                    act.wait_ge(s_st[3], t)
                nc.scalar.activation(neg_maxT[:], score_a[:, 0:64].bitcast(bf16), ACT.Copy).then_inc(s_nmT_sb, 1)

            def exp_group(t, g):
                act.wait_ge(s_st[g], t + 1)
                if g >= 2:
                    act.wait_ge(s_av[g - 2], t + 1)
                elif not first(t):
                    act.wait_ge(s_av[g + 2], t)
                nc.scalar.activation(probs[g % 2], scoreT_of[g][:], ACT.Exp).then_inc(s_ex[g], 1)

            def read_oT(t, n):
                act.wait_ge(s_av[2 * n + 1], t + 1)
                if not first(t):
                    act.wait_ge(s_o, t)
                nc.scalar.activation(oT_sb[:, n * 512:(n + 1) * 512], dense[:, n * 512:(n + 1) * 512],
                                     ACT.Copy).then_inc(s_oT[n], 1)

            def attn_hi(t):
                act.wait_ge(s_aT, t + 1)
                if not first(t):
                    act.wait_ge(s_proj, t)
                nc.scalar.activation(aT_h[:], score_a[:, 0:DIM], ACT.Copy).then_inc(s_aT_h, 1)

            def y_hi(t):
                act.wait_ge(s_yT, t + 1)
                if not first(t):
                    act.wait_ge(s_lg[1], t)
                nc.scalar.activation(yT_h[:], dense[:, 512:1024], ACT.Copy).then_inc(s_yT_h, 1)

            def read_logits(t, n):
                act.wait_ge(s_lg[n], t + 1)
                if not first(t):
                    act.wait_ge(s_rem[0], t)
                    act.wait_ge(s_gexp, t)
                nc.scalar.activation(logit[:, n * 512:(n + 1) * 512], gene[:, n * 512:(n + 1) * 512],
                                     ACT.Copy).then_inc(s_lgr[n], 1)

            def gene_exp(t):
                act.wait_ge(s_ntop, t + 1)
                if not first(t):
                    act.wait_ge(s_wT[1], t)
                nc.scalar.activation(gene_w, logit, ACT.Exp, bias=neg_top[:]).then_inc(s_gexp, 1)

            def read_wT(t, n):
                act.wait_ge(s_wT[n], t + 1)
                if not first(t):
                    act.wait_ge(s_e, t)
                nc.scalar.activation(gene_wT[:, n * 512:(n + 1) * 512], gene[:, n * 512:(n + 1) * 512],
                                     ACT.Copy).then_inc(s_wTr[n], 1)

            def e_hi(t):
                act.wait_ge(s_eT, t + 1)
                if not first(t):
                    act.wait_ge(s_upp, t)
                nc.scalar.activation(eT_h[:], gene[:, 512:512 + P], ACT.Copy).then_inc(s_eT_h, 1)

            def tanh(t):
                act.wait_ge(s_dn, t + 1)
                if not first(t):
                    act.wait_ge(s_y, t)
                nc.scalar.activation(down[:], gene[:, 0:DIM], ACT.Tanh).then_inc(s_tanh, 1)

            def iteration(l, a, b, c, d):
                if a is not None:
                    ctx_hi(a)
                    x_hi(a)
                    read_k(a)
                if c is not None:
                    y_hi(c)
                    read_logits(c, 0)
                if b is not None:
                    read_neg_max(b)
                if a is not None:
                    read_q(a)
                if c is not None:
                    read_logits(c, 1)
                if b is not None:
                    exp_group(b, 0)
                if d is not None:
                    read_wT(d, 0)
                if b is not None:
                    exp_group(b, 1)
                if d is not None:
                    read_wT(d, 1)
                if b is not None:
                    exp_group(b, 2)
                    read_oT(b, 0)
                    exp_group(b, 3)
                if a is not None:
                    split_hi(a, 0)
                if b is not None:
                    read_oT(b, 1)
                if a is not None:
                    read_v(a)
                    split_hi(a, 1)
                if d is not None:
                    e_hi(d)
                if a is not None:
                    read_qkT(a, 0)
                if b is not None:
                    attn_hi(b)
                if a is not None:
                    read_qkT(a, 1)
                if d is not None:
                    tanh(d)
                if a is not None:
                    read_qkT(a, 2)
                if c is not None:
                    gene_exp(c)
                if a is not None:
                    read_qkT(a, 3)

            run(act, iteration)

        @block.vector
        def _(dve):
            steps = [0]

            def step(instruction):
                instruction.then_inc(s_setup, 1)
                steps[0] += 1
                dve.wait_ge(s_setup, steps[0])

            dve.wait_ge(s_small, 16 * 6)
            by_freq = angle[:, 0].rearrange("p (t j) -> p t j", j=4)
            for j, freq in enumerate(ROPE_FREQS):
                last = nc.vector.tensor_scalar(by_freq[:, :, j:j + 1],
                                               pos_sb[:].rearrange("p t (c o) -> p (t c) o", o=1),
                                               freq, None, ALU.mult)
            step(last)
            step(nc.vector.tensor_scalar(turns, angle[:, 0], 1.0 / (TWO_PI_HI + TWO_PI_LO), None, ALU.mult))
            step(nc.vector.scalar_tensor_tensor(angle[:, 0], turns, -TWO_PI_HI, angle[:, 0], ALU.mult, ALU.add))
            step(nc.vector.scalar_tensor_tensor(angle[:, 0], turns, -TWO_PI_LO, angle[:, 0], ALU.mult, ALU.add))
            step(nc.vector.tensor_scalar(angle[:, 0], angle[:, 0], 3.1415925, -3.1415925, ALU.min, ALU.max))
            step(nc.vector.tensor_scalar(angle[:, 2], angle[:, 0], -1.0, None, ALU.mult))
            step(nc.vector.tensor_tensor(angle[:, 1], angle[:, 0], angle[:, 2], ALU.max))
            nc.vector.tensor_scalar(angle[:, 1], angle[:, 1], -1.0, 1.5707963, ALU.mult, ALU.add).then_inc(s_angle, 1)

            step(nc.vector.tensor_scalar(knob[:, 2:3], knob[:, 0:1], 0.1, None, ALU.max))
            step(nc.vector.reciprocal(knob[:, 2:3], knob[:, 2:3]))
            nc.vector.tensor_scalar(wc_scale[:], norm_sb[:], knob[:, 2:3], None, ALU.mult)
            step(nc.vector.tensor_scalar(up_scale[:], norm_sb[:], knob[:, 1:2], None, ALU.mult))
            nc.vector.tensor_copy(knob[:, 3:4], knob[:, 2:3]).then_inc(s_scales, 1)
            dve.wait_ge(s_du, 64)
            nc.vector.tensor_tensor(du_raw[:, 1], du_raw[:, 1],
                                    up_scale[:].unsqueeze(2).broadcast_to([P, XK, 2 * GD]), ALU.mult).then_inc(s_up, 1)

            dve.wait_ge(s_ident, 1)
            nc.vector.tensor_copy(ident16[:], ident[:])
            nc.vector.tensor_copy(identb[:], ident[:])
            step(nc.vector.tensor_tensor(pick[:], ident[:, 0:32], ident[:, 32:64], ALU.add))
            step(nc.vector.tensor_tensor(pick[:], pick[:], ident[:, 64:96], ALU.add))
            step(nc.vector.tensor_tensor(pick[:], pick[:], ident[:, 96:128], ALU.add))
            nc.vector.tensor_copy(select[:], pick[:].unsqueeze(2).broadcast_to([P, HEADS, P]))
            nc.vector.memset(v_ext[:, :, HD:32], 0.0)
            step(nc.vector.memset(parts[:, :, 3], 0.0))
            nc.vector.memset(v_ext[:, :, HD:HD + 1], 1.0).then_inc(s_consts, 1)

            dve.wait_ge(s_act_setup, 1)
            for k in range(XK):
                nc.vector.scalar_tensor_tensor(
                    wq_l[:, k].rearrange("p (two a) -> p two a", two=2),
                    wq_raw[:, k * DIM:(k + 1) * DIM].rearrange("p (a two) -> p two a", two=2), 0.25,
                    wq_h[:, k].bitcast(f32).rearrange("p (two a) -> p two a", two=2), ALU.mult, ALU.subtract)
            for k in range(CK):
                raw = wkv_raw[:, k * 1024:(k + 1) * 1024]
                nc.vector.tensor_tensor(wkv_l[:, k, 0:DIM].rearrange("p (two a) -> p two a", two=2),
                                        raw[:, 0:DIM].rearrange("p (a two) -> p two a", two=2),
                                        wkv_h[:, k, 0:DIM].bitcast(f32).rearrange("p (two a) -> p two a", two=2),
                                        ALU.subtract)
                nc.vector.tensor_tensor(wkv_l[:, k, DIM:1024], raw[:, DIM:1024],
                                        wkv_h[:, k, DIM:1024].bitcast(f32), ALU.subtract)
            nc.vector.tensor_tensor(wout_l[:].rearrange("p k n -> p (k n)"), wout_raw,
                                    wout_h[:].rearrange("p k n -> p (k n)").bitcast(f32),
                                    ALU.subtract).then_inc(s_split, 1)
            for k, bank in enumerate((score_a, score_b, dense, gene)):
                dve.wait_ge(s_wcT_h, k + 1)
                nc.vector.scalar_tensor_tensor(wcT_l[:, k], bank[:], wc_scale[:, k:k + 1],
                                               wcT_h[:, k].bitcast(f32), ALU.mult,
                                               ALU.subtract).then_inc(s_split_wcT, 1)
            dve.wait_ge(s_act_setup, 2)
            nc.vector.tensor_tensor(wduT_l[:], score_a[0:GD, :], wduT_h[0:GD].bitcast(f32),
                                    ALU.subtract).then_inc(s_split_duT, 1)

            def norm1_stats(t):
                hold(dve)
                dve.wait_ge(s_x, (t + 1) * 16)
                nc.vector.bn_stats(bn1[:], slot(t)).then_inc(s_bn1, 1)
                hold(dve)
                dve.wait_ge(s_bn1, t + 1)
                nc.vector.bn_aggr(mv1[:], bn1[:]).then_inc(s_mv1, 1)
                dve.wait_ge(s_mv1, t + 1)
                nc.vector.tensor_scalar(var1[:], mv1[:, 1:2], LN_EPS, None, ALU.add).then_inc(s_var1, 1)

            def norm1_apply(t):
                dve.wait_ge(s_rstd1, t + 1)
                if not first(t):
                    dve.wait_ge(s_xT, t)
                nc.vector.tensor_scalar(xn[:], slot(t), mv1[:, 0:1], rstd1[:], ALU.subtract,
                                        ALU.mult).then_inc(s_xn, 1)

            def ctx_lo(t):
                dve.wait_ge(s_cT_h, t + 1)
                nc.vector.tensor_tensor(cT_l[:], dense[:, 512:512 + CTX], cT_h[:].bitcast(f32),
                                        ALU.subtract).then_inc(s_cT_l, 1)

            def x_lo(t):
                dve.wait_ge(s_xT_h, t + 1)
                nc.vector.tensor_tensor(xT_l[:], dense[:, 0:DIM], xT_h[:].bitcast(f32),
                                        ALU.subtract).then_inc(s_xT_l, 1)

            def group_max(t, g):
                dve.wait_ge(s_sc[g], t + 1)
                if g == 0 and not first(t):
                    dve.wait_ge(s_nml, t)
                nc.vector.tensor_reduce(row_max[:, g * GH:(g + 1) * GH],
                                        score_of[g][:].rearrange("p (s k) -> p s k", k=P),
                                        mybir.AxisListType.X, ALU.max).then_inc(s_mx[g], 1)

            def negate_max(t):
                both = neg_max[:].rearrange("p (r l s) -> p r l s", r=2, l=2)
                maxima = row_max[:].unsqueeze(1).broadcast_to([P, 2, HEADS])
                for g in range(GROUPS):
                    dve.wait_ge(s_mx[g], t + 1)
                if not first(t):
                    dve.wait_ge(s_nmT, t)
                nc.vector.tensor_scalar(both[:, :, 0], maxima, -1.0, None, ALU.mult).then_inc(s_nmh, 1)
                dve.wait_ge(s_nmh, t + 1)
                nc.vector.scalar_tensor_tensor(both[:, :, 1], maxima, -1.0, both[:, :, 0], ALU.mult,
                                               ALU.subtract).then_inc(s_nml, 1)

            def normalise(t):
                o = score_b[:].rearrange("p (h e) -> p h e", e=32)
                dve.wait_ge(s_o, t + 1)
                nc.vector.reciprocal(inv_sum[:].unsqueeze(2), o[:, :, HD:HD + 1]).then_inc(s_inv, 1)
                dve.wait_ge(s_inv, t + 1)
                if not first(t):
                    dve.wait_ge(s_aT, t)
                nc.vector.tensor_tensor(attn[:].rearrange("p (h d) -> p h d", d=HD), o[:, :, 0:HD],
                                        inv_sum[:].unsqueeze(2).broadcast_to([P, HEADS, HD]),
                                        ALU.mult).then_inc(s_attn, 1)

            def attn_lo(t):
                dve.wait_ge(s_aT_h, t + 1)
                nc.vector.tensor_tensor(aT_l[:], score_a[:, 0:DIM], aT_h[:].bitcast(f32),
                                        ALU.subtract).then_inc(s_aT_l, 1)

            def residual(t):
                dve.wait_ge(s_proj, t + 1)
                dve.wait_ge(s_xb, t + 1)
                nc.vector.tensor_tensor(slot(t), score_a[:, 512:1024], slot(t), ALU.add).then_inc(s_x1, 1)

            def norm2_stats(t):
                hold(dve)
                dve.wait_ge(s_x1, t + 1)
                nc.vector.bn_stats(bn2[:], slot(t)).then_inc(s_bn2, 1)
                hold(dve)
                dve.wait_ge(s_bn2, t + 1)
                nc.vector.bn_aggr(mv2[:], bn2[:]).then_inc(s_mv2, 1)
                dve.wait_ge(s_mv2, t + 1)
                nc.vector.tensor_scalar(var2[:], mv2[:, 1:2], 1.0 + RMS_EPS, RMS_EPS * LN_EPS, ALU.mult,
                                        ALU.add).then_inc(s_var2, 1)

            def norm2_apply(t):
                dve.wait_ge(s_norm2, t + 1)
                if not first(t):
                    dve.wait_ge(s_yT, t)
                nc.vector.tensor_scalar(yn[:], slot(t), mv2[:, 0:1], rstd2[:], ALU.subtract,
                                        ALU.mult).then_inc(s_yn, 1)

            def y_lo(t):
                dve.wait_ge(s_yT_h, t + 1)
                nc.vector.tensor_tensor(yT_l[:], dense[:, 512:1024], yT_h[:].bitcast(f32),
                                        ALU.subtract).then_inc(s_yT_l, 1)

            def keep_norm(t):
                dve.wait_ge(s_norm2, t + 1)
                if not first(t):
                    dve.wait_ge(s_t2, t)
                nc.vector.tensor_copy(normx[:, 0:1], mv2[:, 0:1])
                nc.vector.tensor_copy(normx[:, 1:2], rstd2[:]).then_inc(s_normx, 1)

            def find_top(t, n):
                hold(dve)
                if n == 0:
                    dve.wait_ge(s_lgr[0], t + 1)
                    dve.wait_ge(s_lgr[1], t + 1)
                    if not first(t):
                        dve.wait_ge(s_rem[3], t)
                else:
                    dve.wait_ge(s_rem[n - 1], t + 1)
                nc.vector.max(top[:, 8 * n:8 * n + 8], logit if n == 0 else rest).then_inc(s_top[n], 1)

            def remove_top(t, n):
                hold(dve)
                dve.wait_ge(s_top[n], t + 1)
                if n == 0 and not first(t):
                    dve.wait_ge(s_gw, t)
                nc.vector.match_replace(rest, top[:, 8 * n:8 * n + 8], logit if n == 0 else rest,
                                        REMOVED).then_inc(s_rem[n], 1)

            def negate_top(t):
                dve.wait_ge(s_top[0], t + 1)
                if not first(t):
                    dve.wait_ge(s_gexp, t)
                nc.vector.tensor_scalar(neg_top[:], top[:, 0:1], -1.0, None, ALU.mult).then_inc(s_ntop, 1)

            def mask(t):
                dve.wait_ge(s_rem[3], t + 1)
                dve.wait_ge(s_gexp, t + 1)
                nc.vector.scalar_tensor_tensor(gene_w, rest, REMOVED, gene_w, ALU.is_equal, ALU.mult,
                                               accum_out=gene_sum[:]).then_inc(s_gw, 1)
                dve.wait_ge(s_gw, t + 1)
                nc.vector.reciprocal(inv_gene_sum[:], gene_sum[:]).then_inc(s_ginv, 1)

            def scale_e(t):
                dve.wait_ge(s_e, t + 1)
                dve.wait_ge(s_ginv, t + 1)
                if not first(t):
                    dve.wait_ge(s_eT, t)
                nc.vector.tensor_scalar(e_sb[:], gene[:, 0:GD].unsqueeze(1).broadcast_to([P, 2, GD]),
                                        inv_gene_sum[:], None, ALU.mult).then_inc(s_e_sb, 1)

            def e_lo(t):
                dve.wait_ge(s_eT_h, t + 1)
                if not first(t):
                    dve.wait_ge(s_upp, t)
                nc.vector.tensor_copy(eT_hl[0:GD], eT_h[0:GD].bitcast(f32))
                nc.vector.tensor_tensor(eT_hl[GD:2 * GD], gene[GD:2 * GD, 512:512 + P],
                                        eT_h[GD:2 * GD].bitcast(f32), ALU.subtract).then_inc(s_eT_l, 1)

            def combine(t):
                dve.wait_ge(s_tanh, t + 1)
                dve.wait_ge(s_normx, t + 1)
                nc.vector.scalar_tensor_tensor(down[:], slot(t), normx[:, 0:1], down[:], ALU.subtract,
                                               ALU.mult).then_inc(s_t1, 1)
                dve.wait_ge(s_t1, t + 1)
                dve.wait_ge(s_upp, t + 1)
                nc.vector.scalar_tensor_tensor(down[:], down[:], normx[:, 1:2], gene[:, 512:1024], ALU.mult,
                                               ALU.mult).then_inc(s_t2, 1)

            def iteration(l, a, b, c, d):
                if a is not None:
                    ctx_lo(a)
                if b is not None:
                    group_max(b, 0)
                if c is not None:
                    norm2_apply(c)
                if b is not None:
                    group_max(b, 1)
                if a is not None:
                    x_lo(a)
                if c is not None:
                    y_lo(c)
                if b is not None:
                    group_max(b, 2)
                    group_max(b, 3)
                    negate_max(b)
                if d is not None:
                    mask(d)
                if l is not None:
                    norm1_stats(l)
                if c is not None:
                    find_top(c, 0)
                    remove_top(c, 0)
                    negate_top(c)
                    find_top(c, 1)
                    remove_top(c, 1)
                    find_top(c, 2)
                if d is not None:
                    scale_e(d)
                if l is not None:
                    norm1_apply(l)
                if c is not None:
                    remove_top(c, 2)
                if b is not None:
                    normalise(b)
                if d is not None:
                    e_lo(d)
                if c is not None:
                    find_top(c, 3)
                if b is not None:
                    attn_lo(b)
                if c is not None:
                    remove_top(c, 3)
                if d is not None:
                    combine(d)
                if c is not None:
                    keep_norm(c)
                if b is not None:
                    residual(b)
                    norm2_stats(b)

            run(dve, iteration)

        @block.tensor
        def _(pe):
            pe.wait_ge(s_ident, 1)
            pe.wait_ge(s_wc, 16)
            for k, bank in enumerate((score_a, score_b, dense, gene)):
                for g in range(GK):
                    last = nc.tensor.transpose(bank[:, g * P:(g + 1) * P], wc_raw[:, g, k * P:(k + 1) * P], ident[:])
                last.then_inc(s_wcT, 1)
            pe.wait_ge(s_up, 1)
            pe.wait_ge(s_split_wcT, 1)
            for n in range(2):
                for k in range(XK):
                    last = nc.tensor.transpose(score_a[:, n * DIM + k * P:n * DIM + (k + 1) * P],
                                               du_raw[:, n, k], ident[:])
            last.then_inc(s_duT, 1)
            pe.wait_ge(s_consts, 1)
            pe.wait_ge(s_split, 1)
            pe.wait_ge(s_split_wcT, 4)
            pe.wait_ge(s_split_duT, 1)

            def three_pass(out, xs, ws, chunks):
                (xh, xl), (wh, wl) = xs, ws
                n, steps = 0, 3 * chunks
                for k in range(chunks):
                    for lhs, rhs in ((xh, wh), (xh, wl), (xl, wh)):
                        last = nc.tensor.matmul(out, lhs[:, k * P:(k + 1) * P], rhs(k), start=(n == 0),
                                                stop=(n == steps - 1))
                        n += 1
                return last

            def columns(w, at):
                return lambda k: w[:, k, at:at + 512]

            def transpose_x(t):
                pe.wait_ge(s_xn, t + 1)
                if not first(t):
                    pe.wait_ge(s_trr[2], t)
                for k in range(XK):
                    last = nc.tensor.transpose(dense[:, k * P:(k + 1) * P], xn[:, k * P:(k + 1) * P], ident[:])
                last.then_inc(s_xT, 1)

            def transpose_ctx(t):
                pe.wait_ge(s_ctx, (t + 1) * 16)
                if not first(t):
                    pe.wait_ge(s_trr[3], t)
                for k in range(CK):
                    last = nc.tensor.transpose(dense[:, 512 + k * P:512 + (k + 1) * P],
                                               ctx_sb[:, k * P:(k + 1) * P], ident[:])
                last.then_inc(s_cT, 1)

            def project_q(t):
                pe.wait_ge(s_xT_h, t + 1)
                pe.wait_ge(s_xT_l, t + 1)
                three_pass(dense[:, 0:512], (xT_h, xT_l), (columns(wq_h, 0), columns(wq_l, 0)),
                           XK).then_inc(s_q, 1)

            def project_k(t):
                pe.wait_ge(s_cT_h, t + 1)
                pe.wait_ge(s_cT_l, t + 1)
                three_pass(dense[:, 512:1024], (cT_h, cT_l), (columns(wkv_h, 0), columns(wkv_l, 0)),
                           CK).then_inc(s_k, 1)

            def project_v(t):
                pe.wait_ge(s_q_sb, t + 1)
                if not first(t):
                    pe.wait_ge(s_oT[0], t)
                three_pass(dense[:, 0:512], (cT_h, cT_l), (columns(wkv_h, 512), columns(wkv_l, 512)),
                           CK).then_inc(s_v, 1)

            def transpose_qk(t, n):
                if n == 0:
                    pe.wait_ge(s_hi[0], t + 1)
                    pe.wait_ge(s_lo[0], t + 1)
                    pe.wait_ge(s_v_sb, t + 1)
                elif n == 1:
                    pe.wait_ge(s_k_sb, t + 1)
                    if not first(t):
                        pe.wait_ge(s_oT[1], t)
                else:
                    if n == 2:
                        pe.wait_ge(s_hi[1], t + 1)
                        pe.wait_ge(s_lo[1], t + 1)
                    pe.wait_ge(s_trr[n - 2], t + 1)
                half = dense[:, (n % 2) * 512:(n % 2 + 1) * 512].bitcast(f16)
                for m in range(8):
                    last = nc.tensor.transpose(half[:, m * P:(m + 1) * P],
                                               pair_in(n // 2, (n % 2) * 8 + m), ident16[:])
                last.then_inc(s_tr[n], 1)

            def scores(t, g):
                if g == 0:
                    for n in range(4):
                        pe.wait_ge(s_trr[n], t + 1)
                    if not first(t):
                        pe.wait_ge(s_x1, t)
                elif g == 1:
                    if not first(t):
                        pe.wait_ge(s_attn, t)
                else:
                    pe.wait_ge(s_mx[g - 2], t + 1)
                for r in range(GH):
                    head = g * GH + r
                    at = (r % 2) * 512 + (r // 2) * P
                    last = nc.tensor.matmul(score_of[g][:, at:at + P], rows_of(qT, head), rows_of(kT, head),
                                            start=True, stop=True)
                last.then_inc(s_sc[g], 1)

            def transpose_neg_max(t):
                pe.wait_ge(s_nmh, t + 1)
                pe.wait_ge(s_nml, t + 1)
                nc.tensor.transpose(score_a[:, 0:64].bitcast(bf16), neg_max[:], identb[:]).then_inc(s_nmT, 1)

            def scoresT(t, g):
                if g == 0:
                    pe.wait_ge(s_mx[3], t + 1)
                elif g == 1:
                    pe.wait_ge(s_nmT_sb, t + 1)
                else:
                    pe.wait_ge(s_ex[g - 2], t + 1)
                if g == 0:
                    pe.wait_ge(s_nmT_sb, t + 1)
                for r in range(0, GH, 2):
                    for step in range(2):
                        for odd in range(2):
                            head = g * GH + r + odd
                            at = odd * 512 + (r // 2) * P
                            out = scoreT_of[g][:, at:at + P]
                            if step == 0:
                                nc.tensor.matmul(out, rows_of(kT, head), rows_of(qT, head), start=True, stop=False)
                            else:
                                rows = slice(64 * odd, 64 * odd + 64)
                                place = g * GH + odd * 4 + r // 2
                                last = nc.tensor.matmul(out, select[rows, place], neg_maxT[rows, :],
                                                        start=False, stop=True)
                last.then_inc(s_st[g], 1)

            def values(t, g):
                if g == 0:
                    pe.wait_ge(s_v_sb, t + 1)
                    if not last_tile(t):
                        pe.wait_ge(s_q_sb, t + 2)
                elif g == 2 and not first(t):
                    pe.wait_ge(s_yT_l, t)
                pe.wait_ge(s_ex[g], t + 1)
                for r in range(GH):
                    head = g * GH + r
                    rows = slice(32 * (r % 4), 32 * (r % 4) + 32)
                    at = (2 * g + r // 4) * P
                    slot_at = ((r % 2) * 4 + r // 2) * P
                    last = nc.tensor.matmul(dense[rows, at:at + P], v_ext[:, head], probs[g % 2][:, slot_at:slot_at + P],
                                            start=True, stop=True)
                last.then_inc(s_av[g], 1)

            def transpose_o(t):
                pe.wait_ge(s_oT[0], t + 1)
                pe.wait_ge(s_oT[1], t + 1)
                pe.wait_ge(s_ex[2], t + 1)
                for n in range(8):
                    last = nc.tensor.transpose(score_b[:, n * P:(n + 1) * P], oT_sb[:, n * P:(n + 1) * P], ident[:])
                last.then_inc(s_o, 1)

            def transpose_attn(t):
                pe.wait_ge(s_attn, t + 1)
                pe.wait_ge(s_ex[3], t + 1)
                for k in range(XK):
                    last = nc.tensor.transpose(score_a[:, k * P:(k + 1) * P], attn[:, k * P:(k + 1) * P], ident[:])
                last.then_inc(s_aT, 1)

            def project_out(t):
                pe.wait_ge(s_aT_h, t + 1)
                pe.wait_ge(s_aT_l, t + 1)
                three_pass(score_a[:, 512:1024], (aT_h, aT_l), (columns(wout_h, 0), columns(wout_l, 0)),
                           XK).then_inc(s_proj, 1)

            def transpose_y(t):
                pe.wait_ge(s_yn, t + 1)
                if not (isinstance(t, int) and t + 2 >= TILES):
                    pe.wait_ge(s_k_sb, t + 3)
                for k in range(XK):
                    last = nc.tensor.transpose(dense[:, 512 + k * P:512 + (k + 1) * P], yn[:, k * P:(k + 1) * P], ident[:])
                last.then_inc(s_yT, 1)

            def logits(t, n):
                if n == 0:
                    pe.wait_ge(s_yT_h, t + 1)
                    pe.wait_ge(s_yT_l, t + 1)
                if not isinstance(t, int) or t >= 2:
                    pe.wait_ge((s_tanh, s_t2)[n], t - 1)
                three_pass(gene[:, n * 512:(n + 1) * 512], (yT_h, yT_l),
                           (columns(wcT_h, n * 512), columns(wcT_l, n * 512)), XK).then_inc(s_lg[n], 1)

            def transpose_w(t, n):
                pe.wait_ge(s_gw, t + 1)
                if last_tile(t):
                    pe.wait_ge((s_tanh, s_t2)[n], t)
                else:
                    pe.wait_ge(s_lgr[n], t + 2)
                for g in range(4 * n, 4 * n + 4):
                    last = nc.tensor.transpose(gene[:, g * P:(g + 1) * P], gene_w[:, g * P:(g + 1) * P], ident[:])
                last.then_inc(s_wT[n], 1)

            def express(t):
                pe.wait_ge(s_wTr[0], t + 1)
                pe.wait_ge(s_wTr[1], t + 1)
                for g in range(GK):
                    last = nc.tensor.matmul(gene[:, 0:GD], gene_wT[:, g * P:(g + 1) * P], genes_sb[:, g],
                                            start=(g == 0), stop=(g == GK - 1))
                last.then_inc(s_e, 1)

            def transpose_e(t):
                pe.wait_ge(s_e_sb, t + 1)
                nc.tensor.transpose(gene[:, 512:512 + P], e_sb[:].rearrange("p r c -> p (r c)"), ident[:]).then_inc(s_eT, 1)

            def down_up(t):
                pe.wait_ge(s_eT_h, t + 1)
                pe.wait_ge(s_eT_l, t + 1)
                for n, done in enumerate((s_dn, s_upp)):
                    cols = slice(n * DIM, (n + 1) * DIM)
                    nc.tensor.matmul(gene[:, cols], eT_hl[:], wduT_h[:, cols], start=True, stop=False)
                    nc.tensor.matmul(gene[:, cols], eT_h[0:GD], wduT_l[:, cols], start=False,
                                     stop=True).then_inc(done, 1)

            def iteration(l, a, b, c, d):
                if a is not None:
                    transpose_ctx(a)
                if b is not None:
                    scores(b, 0)
                if a is not None:
                    transpose_x(a)
                if b is not None:
                    scores(b, 1)
                if a is not None:
                    project_k(a)
                if b is not None:
                    scores(b, 2)
                if c is not None:
                    transpose_y(c)
                if b is not None:
                    scores(b, 3)
                if a is not None:
                    project_q(a)
                if c is not None:
                    logits(c, 0)
                if b is not None:
                    transpose_neg_max(b)
                if c is not None:
                    logits(c, 1)
                if b is not None:
                    scoresT(b, 0)
                if d is not None:
                    transpose_w(d, 0)
                if b is not None:
                    scoresT(b, 1)
                if d is not None:
                    transpose_w(d, 1)
                if b is not None:
                    values(b, 0)
                    scoresT(b, 2)
                    values(b, 1)
                    scoresT(b, 3)
                    values(b, 2)
                if d is not None:
                    express(d)
                if b is not None:
                    values(b, 3)
                if a is not None:
                    project_v(a)
                if b is not None:
                    transpose_o(b)
                if a is not None:
                    transpose_qk(a, 0)
                if d is not None:
                    transpose_e(d)
                if a is not None:
                    transpose_qk(a, 1)
                if b is not None:
                    transpose_attn(b)
                if a is not None:
                    transpose_qk(a, 2)
                if d is not None:
                    down_up(d)
                if b is not None:
                    project_out(b)
                if a is not None:
                    transpose_qk(a, 3)

            run(pe, iteration)


NAMES = ['x', 'ctx_1024', 'fside_BxSx2_0', 'L0_xattn_Wq', 'L0_xattn_Wkv', 'L0_xattn_Wout', 'L0_xattn_bout',
         'L0_ffn_Wc', 'L0_ffn_temperature', 'L0_ffn_genes', 'L0_ffn_Wd', 'L0_ffn_Wu', 'L0_ffn_norm_w',
         'L0_ffn_scale']


def kernel(**inputs):
    import numpy as np
    import concourse.bacc as bacc
    from concourse.bass_utils import run_bass_kernel_spmd

    nc = bacc.Bacc("TRN2", target_bir_lowering=False, num_devices=1)
    arrays, args = {}, []
    for name in NAMES:
        a = np.ascontiguousarray(inputs[name])
        a = a.reshape(a.shape or (1,))
        if name == 'L0_ffn_norm_w':
            a = np.ascontiguousarray(a.reshape(XK, P).T)
        arrays[name + "_dram"] = a
        args.append(nc.dram_tensor(name + "_dram", a.shape, mybir.dt.from_np(a.dtype), kind="ExternalInput").ap())
    out = nc.dram_tensor("out_dram", (TILES, P, DIM), f32, kind="ExternalOutput").ap()
    build(nc, *args, out)
    result = run_bass_kernel_spmd(nc, [arrays], core_ids=[0])
    return result.results[0]["out_dram"]
```

```python
from contextlib import ExitStack

import concourse.bass as bass
from concourse import mybir

P = 128
TILES = 16
DIM, CTX = 512, 256
HEADS, HD = 32, 16
GENES, GD = 1024, 64
TOP = 32
XK, CK, GK = DIM // P, CTX // P, GENES // P
XSLOTS = 6
GROUPS = 4
GH = HEADS // GROUPS
LN_EPS = 1e-5
RMS_EPS = 2.0 ** -23
UNIT = 2048.0
REMOVED = -3.0e38
ROPE_FREQS = [10000.0 ** (-j / 4) for j in range(4)]
TWO_PI_HI, TWO_PI_LO = 6.28125, 6.283185307179586 - 6.28125

f32, f32r = mybir.dt.float32, mybir.dt.float32r
f16, i32 = mybir.dt.float16, mybir.dt.int32
ALU = mybir.AluOpType
ACT = mybir.ActivationFunctionType


def build(nc, x, ctx, pos, wq, wkv, wout, bout, wc, temp, genes, wd, wu, norm_w, scale, out):
    stack = ExitStack()
    with stack:
        def sb(name, shape, dt=f32):
            return stack.enter_context(nc.sbuf_tensor(name, shape, dt))

        def ps(name):
            return stack.enter_context(nc.psum_tensor(name, [P, 1024], f32))

        def sem(name):
            return stack.enter_context(nc.semaphore(name))

        wq_h, wq_l = sb("wq_h", [P, XK, DIM], f32r), sb("wq_l", [P, XK, DIM], f32r)
        wkv_h, wkv_l = sb("wkv_h", [P, CK, 2 * DIM], f32r), sb("wkv_l", [P, CK, 2 * DIM], f32r)
        wout_h, wout_l = sb("wout_h", [P, XK, DIM], f32r), sb("wout_l", [P, XK, DIM], f32r)
        wcT_h, wcT_l = sb("wcT_h", [P, XK, GENES], f32r), sb("wcT_l", [P, XK, GENES], f32r)
        wduT_h, wduT_l = sb("wduT_h", [2 * GD, 2 * DIM], f32r), sb("wduT_l", [GD, 2 * DIM], f32r)
        genes_sb = sb("genes_sb", [P, GK, 2 * GD])
        du_raw = sb("du_raw", [P, 2, XK, 2 * GD])
        bout_sb = sb("bout_sb", [P, DIM])
        norm_sb = sb("norm_sb", [P, XK])
        wc_scale = sb("wc_scale", [P, XK])
        up_scale = sb("up_scale", [P, XK])
        knob = sb("knob", [P, 4])
        minus_half = sb("minus_half", [P, 1])
        ident = sb("ident", [P, P])
        ident16 = sb("ident16", [P, P], f16)
        pos_raw = sb("pos_raw", [TILES, 2 * P])
        cos_t, sin_t = sb("cos_t", [P, TILES * 8]), sb("sin_t", [P, TILES * 8])

        stage_a = sb("stage_a", [P, 4096])
        stage_b = sb("stage_b", [P, 6144])
        wc_raw = stage_a[:, :].rearrange("p (g d) -> p g d", d=DIM)
        wkv_raw = stage_b[:, 0:2048]
        wq_raw = stage_b[:, 2048:4096]
        wout_raw = stage_b[:, 4096:6144]
        probs = [stage_a[:, 0:1024], stage_a[:, 1024:2048]]
        gene_w = stage_a[:, 2048:3072]
        gene_wT = stage_a[:, 3072:4096]
        qk_sb = stage_b[:, 0:1024]
        qk_cos, qk_sin = stage_b[:, 1024:2048], stage_b[:, 2048:3072]
        logit = stage_b[:, 3072:4096]
        rest = stage_b[:, 4096:5120]
        oT_sb = stage_b[:, 5120:6144]

        x_ring = sb("x_ring", [P, XSLOTS * DIM])
        ctx_sb = sb("ctx_sb", [P, CTX])
        xn = sb("xn", [P, DIM])
        xT_h, xT_l = sb("xT_h", [P, DIM], f32r), sb("xT_l", [P, DIM], f32r)
        cT_h, cT_l = sb("cT_h", [P, CTX], f32r), sb("cT_l", [P, CTX], f32r)
        turned = sb("turned", [P, 2 * DIM])
        parts = sb("parts", [P, 2 * HEADS, 4, HD], f16)
        qT, kT = sb("qT", [P, HEADS // 2 * P], f16), sb("kT", [P, HEADS // 2 * P], f16)
        v_ext = sb("v_ext", [P, HEADS, 32])
        attn = sb("attn", [P, DIM])
        aT_h, aT_l = sb("aT_h", [P, DIM], f32r), sb("aT_l", [P, DIM], f32r)
        yn = sb("yn", [P, DIM])
        angle = attn[:, 0:3 * TILES * 8].rearrange("p (n a) -> p n a", n=3)
        turns = yn[:, 0:TILES * 8].bitcast(i32)
        yT_h, yT_l = sb("yT_h", [P, DIM], f32r), sb("yT_l", [P, DIM], f32r)
        down = sb("down", [P, DIM])
        row_max = sb("row_max", [P, HEADS])
        neg_max = sb("neg_max", [P, P], f16)
        neg_maxT = sb("neg_maxT", [P, P], f16)
        inv_sum = sb("inv_sum", [P, HEADS])
        bn1, bn2 = sb("bn1", [P, 6]), sb("bn2", [P, 6])
        mv1, mv2 = sb("mv1", [P, 2]), sb("mv2", [P, 2])
        var1, rstd1 = sb("var1", [P, 1]), sb("rstd1", [P, 1])
        var2, rstd2 = sb("var2", [P, 1]), sb("rstd2", [P, 1])
        normx = sb("normx", [P, 2])
        top = sb("top", [P, TOP])
        neg_top = sb("neg_top", [P, 1])
        gene_sum, inv_gene_sum = sb("gene_sum", [P, 1]), sb("inv_gene_sum", [P, 1])
        up_factor = sb("up_factor", [P, 1])
        eT_h = sb("eT_h", [2 * GD, P], f32r)
        eT_hl = sb("eT_hl", [2 * GD, P], f32r)

        score_a, score_b, dense, gene = ps("score_a"), ps("score_b"), ps("dense"), ps("gene")

        s_wq, s_wkv, s_wout, s_wc, s_du, s_small, s_genes, s_pos = (sem(n) for n in (
            "wq_in", "wkv_in", "wout_in", "wc_in", "du_in", "small_in", "genes_in", "pos_in"))
        s_posT = sem("pos_in_psum")
        s_ident = sem("ident_ready")
        s_pool_setup = sem("pool_setup")
        s_setup = sem("dve_setup")
        s_wq_h, s_wkv_h, s_wout_h, s_duT_h = (sem(n) for n in ("wq_h_done", "wkv_h_done", "wout_h_done", "duT_h_done"))
        s_wcT = sem("wcT_in_psum")
        s_duT = sem("duT_in_psum")
        s_trig = sem("trig_ready")
        s_angle, s_scales, s_consts, s_up = (sem(n) for n in (
            "angles_ready", "scales_ready", "constants_ready", "up_weights_scaled"))
        s_split_kv, s_split_q, s_split_out = sem("wkv_split"), sem("wq_split"), sem("wout_split")
        s_split_wcT, s_split_duT = sem("wcT_split"), sem("duT_split")
        s_wcT_h = sem("wcT_h_done")
        s_x, s_ctx = sem("x_loaded"), sem("ctx_loaded")
        s_bn1, s_mv1, s_var1, s_rstd1, s_xn = (sem(n) for n in (
            "bn1_done", "mv1_done", "var1_done", "rstd1_done", "xn_done"))
        s_xT, s_cT = sem("xT_in_psum"), sem("cT_in_psum")
        s_xT_h, s_xT_l, s_cT_h, s_cT_l = (sem(n) for n in ("xT_h_done", "xT_l_done", "cT_h_done", "cT_l_done"))
        s_q, s_k, s_v = sem("q_in_psum"), sem("k_in_psum"), sem("v_in_psum")
        s_q_sb, s_k_sb, s_v_sb = sem("q_read"), sem("k_read"), sem("v_read")
        s_cosm, s_sinm, s_rot, s_hi, s_lo = ([sem(f"{x}_{what}") for x in "qk"] for what in (
            "cos_done", "sin_done", "rope_done", "hi_done", "lo_done"))
        s_xb = sem("bout_added")
        s_tr = [sem(f"qkT{n}_in_psum") for n in range(4)]
        s_trr = [sem(f"qkT{n}_read") for n in range(4)]
        s_sc = [sem(f"scores{g}_in_psum") for g in range(GROUPS)]
        s_mx = [sem(f"max{g}_done") for g in range(GROUPS)]
        s_nmh, s_nml = sem("neg_max_hi_done"), sem("neg_max_lo_done")
        s_nmT, s_nmT_sb, s_shift = sem("neg_maxT_in_psum"), sem("neg_maxT_read"), sem("neg_max_in_qT")
        s_st = [sem(f"scoresT{g}_in_psum") for g in range(GROUPS)]
        s_ex = [sem(f"exp{g}_done") for g in range(GROUPS)]
        s_av = [sem(f"values{g}_done") for g in range(GROUPS)]
        s_oT = [sem(f"oT{n}_read") for n in range(2)]
        s_o, s_inv, s_attn = sem("o_in_psum"), sem("inv_sum_done"), sem("attn_done")
        s_aT, s_aT_h, s_aT_l = sem("attnT_in_psum"), sem("attnT_h_done"), sem("attnT_l_done")
        s_proj, s_x1 = sem("proj_in_psum"), sem("x1_done")
        s_bn2, s_mv2, s_var2, s_norm2, s_yn = (sem(n) for n in (
            "bn2_done", "mv2_done", "var2_done", "norm2_done", "yn_done"))
        s_mean2 = sem("mean2_copied")
        s_yT, s_yT_h, s_yT_l = sem("ynT_in_psum"), sem("ynT_h_done"), sem("ynT_l_done")
        s_normx = sem("norm_copied")
        s_lg = [sem(f"logits{n}_in_psum") for n in range(2)]
        s_lgr = [sem(f"logits{n}_read") for n in range(2)]
        s_top = [sem(f"top{n}_found") for n in range(4)]
        s_rem = [sem(f"top{n}_removed") for n in range(4)]
        s_ntop, s_gexp, s_gw, s_ginv = (sem(n) for n in ("neg_top_done", "gene_exp_done", "gene_w_done", "inv_gene_sum_done"))
        s_wT = [sem(f"gene_wT{n}_in_psum") for n in range(2)]
        s_wTr = [sem(f"gene_wT{n}_read") for n in range(2)]
        s_upf, s_eT, s_eT_h, s_eT_l = (sem(n) for n in ("up_factor_done", "eT_in_psum", "eT_h_done", "eT_l_done"))
        s_dn, s_upp, s_tanh, s_t1, s_t2, s_y = (sem(n) for n in (
            "down_in_psum", "up_in_psum", "tanh_done", "t1_done", "t2_done", "y_done"))
        s_out = sem("out_stored")

        def slot(t):
            if isinstance(t, int):
                return x_ring[:, (t % XSLOTS) * DIM:(t % XSLOTS + 1) * DIM]
            return x_ring[:, bass.ds((t % XSLOTS) * DIM, DIM)]

        def trig(table, t):
            at = table[:, t * 8:(t + 1) * 8] if isinstance(t, int) else table[:, bass.ds(t * 8, 8)]
            return at.unsqueeze(1).broadcast_to([P, 2 * HEADS, 8])

        q_parts, k_parts = parts[:, 0:HEADS], parts[:, HEADS:2 * HEADS]

        def head_major(t, n):
            return t[:, n * DIM:(n + 1) * DIM].rearrange("p (h d) -> p h d", d=HD)

        def pair_in(n, m):
            at = n * HEADS + 2 * m
            return parts[:, at:at + 2].rearrange("p h l d -> p (h l d)")

        def rows_of(t, head):
            r = 64 * (head % 2)
            return t[r:r + 64, (head // 2) * P:(head // 2 + 1) * P]

        wcT_bank = (score_a, score_b, gene, score_a)
        score_of = [score_a, score_b, score_a, score_b]
        scoreT_of = [score_b, score_a, score_b, score_a]

        block = stack.enter_context(nc.Block())

        def last_tile(t):
            return isinstance(t, int) and t == TILES - 1

        def first(t):
            return isinstance(t, int) and t == 0

        def hold(eng):
            eng.wait_ge(s_trig, 1)

        def run(eng, begin, filling, iteration, draining):
            begin()
            for i in range(2, 5):
                filling(*(i - n if i >= n else None for n in range(5)))
            with eng.Fori(5, TILES) as i:
                iteration(i, i - 1, i - 2, i - 3, i - 4)
            for i in range(TILES, TILES + 4):
                draining(*(i - n if i - n < TILES else None for n in range(5)))

        @block.sync
        def _(sp):
            def load_x(t):
                if isinstance(t, int):
                    src = x[t]
                else:
                    src = x[bass.ds(t, 1)].rearrange("o p n -> p (o n)")
                sp.dma_start(slot(t), src).then_inc(s_x, 16)

            def load_ctx(t):
                if isinstance(t, int):
                    src = ctx[t]
                else:
                    src = ctx[bass.ds(t, 1)].rearrange("o p n -> p (o n)")
                sp.dma_start(ctx_sb[:], src).then_inc(s_ctx, 16)

            def store(t):
                sp.wait_ge(s_y, t + 1)
                if isinstance(t, int):
                    dst = out[t]
                else:
                    dst = out[bass.ds(t, 1)].rearrange("o p n -> p (o n)")
                sp.dma_start(dst, slot(t)).then_inc(s_out, 16)

            sp.dma_start(pos_raw[:], pos.rearrange("t p c -> t (p c)")).then_inc(s_pos, 16)
            load_x(0)
            load_ctx(0)
            sp.dma_start(wkv_raw, wkv.rearrange("(k p) n -> p k n", p=P)).then_inc(s_wkv, 16)
            sp.dma_start(wc_raw, wc.rearrange("(g p) d -> p g d", p=P)).then_inc(s_wc, 16)

            def next_x(t):
                loaded, stored = (t + 1) * 16, (t + 2 - XSLOTS) * 16
                sp.wait_ge(s_x, loaded)
                if not isinstance(t, int) or t >= XSLOTS:
                    sp.wait_ge(s_out, stored)
                load_x(t + 1)

            def next_ctx(t):
                sp.wait_ge(s_cT, t + 1)
                load_ctx(t + 1)

            def shift(t):
                sp.wait_ge(s_nmT_sb, t + 1)
                for odd in range(2):
                    sp.dma_start(qT[64 * odd + 48:64 * odd + 50, :],
                                 neg_maxT[odd * HEADS:(odd + 1) * HEADS, :]).then_inc(s_shift, 16)

            def iteration(l, a, b, c, d):
                if l is not None and not (isinstance(l, int) and l == TILES - 1):
                    next_x(l)
                if a is not None and not (isinstance(a, int) and a == TILES - 1):
                    next_ctx(a)
                if b is not None:
                    shift(b)
                if d is not None:
                    store(d)

            for i in range(XSLOTS):
                iteration(*(i - n if i >= n else None for n in range(5)))
            with sp.Fori(XSLOTS, TILES - 1) as i:
                iteration(i, i - 1, i - 2, i - 3, i - 4)
            for i in range(TILES - 1, TILES + 4):
                iteration(*(i - n if i - n < TILES else None for n in range(5)))
            sp.wait_ge(s_out, TILES * 16)

        @block.gpsimd
        def _(pool):
            pool.memset(ident[:], 0.0).then_inc(s_pool_setup, 1)
            pool.wait_ge(s_pool_setup, 1)
            pool.affine_select(out=ident[:], in_=ident[:], compare_op=ALU.not_equal, fill=1.0, base=0,
                               pattern=[[-1, P]], channel_multiplier=1).then_inc(s_ident, 1)
            pool.memset(minus_half[:], -0.5).then_inc(s_pool_setup, 1)
            pool.wait_ge(s_pool_setup, 2)

            def ln1(t):
                pool.wait_ge(s_var1, t + 1)
                pool.tensor_tensor(rstd1[:], var1[:], minus_half[:], ALU.pow).then_inc(s_rstd1, 1)

            def add_bout(t):
                hold(pool)
                pool.wait_ge(s_xn, t + 1)
                pool.tensor_tensor(slot(t), slot(t), bout_sb[:], ALU.add).then_inc(s_xb, 1)

            def rope(t, n):
                def halves(m):
                    return m[:, n * DIM:(n + 1) * DIM].rearrange("p (a j) -> p a j", j=8)

                hold(pool)
                pool.wait_ge((s_q_sb, s_k_sb)[n], t + 1)
                if not first(t):
                    pool.wait_ge(s_rot[n], t)
                pool.tensor_tensor(halves(qk_cos), halves(qk_sb), trig(cos_t, t), ALU.mult).then_inc(s_cosm[n], 1)
                pool.tensor_tensor(halves(qk_sin), halves(qk_sb), trig(sin_t, t), ALU.mult).then_inc(s_sinm[n], 1)

            def rope_sum(t, n):
                c = qk_cos[:, n * DIM:(n + 1) * DIM].rearrange("p (two h j) -> p two h j", two=2, j=8)
                s = qk_sin[:, n * DIM:(n + 1) * DIM].rearrange("p (two h j) -> p two h j", two=2, j=8)
                o = turned[:, n * DIM:(n + 1) * DIM].rearrange("p (h two j) -> p h two j", two=2, j=8)
                pool.wait_ge(s_cosm[n], t + 1)
                pool.wait_ge(s_sinm[n], t + 1)
                if not first(t):
                    pool.wait_ge(s_hi[n], t)
                    pool.wait_ge(s_lo[n], t)
                pool.tensor_tensor(o[:, :, 0], c[:, 0], s[:, 1], ALU.subtract)
                pool.tensor_tensor(o[:, :, 1], c[:, 1], s[:, 0], ALU.add).then_inc(s_rot[n], 1)

            def split_lo(t, n):
                pool.wait_ge(s_rot[n], t + 1)
                pool.wait_ge(s_hi[n], t + 1)
                if not first(t):
                    pool.wait_ge(s_tr[2 * n + 1], t)
                to = (q_parts[:, :, 1], k_parts[:, :, 2])[n]
                pool.tensor_tensor(to, head_major(turned, n), (q_parts, k_parts)[n][:, :, 0],
                                   ALU.subtract).then_inc(s_lo[n], 1)

            def ln2(t):
                pool.wait_ge(s_var2, t + 1)
                if not first(t):
                    pool.wait_ge(s_normx, t)
                pool.tensor_tensor(rstd2[:], var2[:], minus_half[:], ALU.pow).then_inc(s_norm2, 1)

            def finish(t):
                hold(pool)
                pool.wait_ge(s_t2, t + 1)
                pool.tensor_tensor(slot(t), slot(t), down[:], ALU.add).then_inc(s_y, 1)

            pool.wait_ge(s_trig, 1)

            def iteration(l, a, b, c, d):
                if a is not None:
                    add_bout(a)
                    rope(a, 1)
                    rope(a, 0)
                    rope_sum(a, 0)
                    rope_sum(a, 1)
                    split_lo(a, 0)
                    split_lo(a, 1)
                if d is not None:
                    finish(d)
                if l is not None:
                    ln1(l)
                if b is not None:
                    ln2(b)

            filling = iteration

            def draining(l, a, b, c, d):
                if a is not None:
                    rope(a, 1)
                    rope(a, 0)
                    rope_sum(a, 0)
                    rope_sum(a, 1)
                    split_lo(a, 0)
                    add_bout(a)
                    split_lo(a, 1)
                if d is not None:
                    finish(d)
                if b is not None:
                    ln2(b)

            def begin():
                ln1(0)
                pool.wait_ge(s_split_q, 1)
                rope(0, 1)
                rope_sum(0, 1)
                ln1(1)
                rope(0, 0)
                rope_sum(0, 0)
                split_lo(0, 1)
                split_lo(0, 0)
                pool.wait_ge(s_small, 16 * 4)
                add_bout(0)

            run(pool, begin, filling, iteration, draining)

        @block.scalar
        def _(act):
            act.dma_start(wq_raw, wq.rearrange("(k p) n -> p k n", p=P)).then_inc(s_wq, 16)
            act.dma_start(norm_sb[:], norm_w).then_inc(s_small, 16)
            act.dma_start(knob[:, 0:1], temp.rearrange("(o n) -> o n", o=1).broadcast_to([P, 1])).then_inc(s_small, 16)
            act.dma_start(knob[:, 1:2], scale.rearrange("(o n) -> o n", o=1).broadcast_to([P, 1])).then_inc(s_small, 16)
            act.dma_start(bout_sb[:], bout.rearrange("(o n) -> o n", o=1).broadcast_to([P, DIM])).then_inc(s_small, 16)
            act.dma_start(wout_raw, wout.rearrange("(k p) n -> p k n", p=P)).then_inc(s_wout, 16)
            for half in range(2):
                cols = slice(half * GD, (half + 1) * GD)
                for n, w in enumerate((wd, wu)):
                    act.dma_start(du_raw[:, n, :, cols], w.rearrange("(k p) c -> p k c", p=P)).then_inc(s_du, 16)
                act.dma_start(genes_sb[:, :, cols], genes.rearrange("(g p) c -> p g c", p=P)).then_inc(s_genes, 16)

            act.wait_ge(s_angle, 1)
            nc.scalar.activation(sin_t[:], angle[:, 0], ACT.Sin)
            nc.scalar.activation(cos_t[:], angle[:, 1], ACT.Sin).then_inc(s_trig, 1)

            act.wait_ge(s_wkv, 16)
            for k in range(CK):
                raw = wkv_raw[:, k * 1024:(k + 1) * 1024]
                nc.scalar.activation(wkv_h[:, k, 0:DIM].rearrange("p (two a) -> p two a", two=2),
                                     raw[:, 0:DIM].rearrange("p (a two) -> p two a", two=2), ACT.Copy)
                last = nc.scalar.activation(wkv_h[:, k, DIM:1024], raw[:, DIM:1024], ACT.Copy)
            last.then_inc(s_wkv_h, 1)
            act.wait_ge(s_wq, 16)
            for k in range(XK):
                last = nc.scalar.activation(
                    wq_h[:, k].rearrange("p (two a) -> p two a", two=2),
                    wq_raw[:, k * DIM:(k + 1) * DIM].rearrange("p (a two) -> p two a", two=2),
                    ACT.Copy, scale=0.25)
            last.then_inc(s_wq_h, 1)

            def wout_hi():
                act.wait_ge(s_wout, 16)
                nc.scalar.activation(wout_h[:].rearrange("p k n -> p (k n)"), wout_raw,
                                     ACT.Copy).then_inc(s_wout_h, 1)

            def wcT_hi(k):
                act.wait_ge(s_scales, 1)
                act.wait_ge(s_wcT, k + 1)
                nc.scalar.activation(wcT_h[:, k], wcT_bank[k][:], ACT.Copy,
                                     scale=wc_scale[:, k:k + 1]).then_inc(s_wcT_h, 1)

            def duT_hi():
                act.wait_ge(s_duT, 1)
                nc.scalar.activation(wduT_h[:], score_b[:], ACT.Copy).then_inc(s_duT_h, 1)

            def ctx_hi(t):
                act.wait_ge(s_cT, t + 1)
                if not first(t):
                    act.wait_ge(s_v, t)
                nc.scalar.activation(cT_h[:], dense[:, 512:512 + CTX], ACT.Copy).then_inc(s_cT_h, 1)

            def x_hi(t):
                act.wait_ge(s_xT, t + 1)
                if not first(t):
                    act.wait_ge(s_q, t)
                nc.scalar.activation(xT_h[:], dense[:, 0:DIM], ACT.Copy).then_inc(s_xT_h, 1)

            def read_q(t):
                act.wait_ge(s_q, t + 1)
                if not first(t):
                    act.wait_ge(s_cosm[0], t)
                    act.wait_ge(s_sinm[0], t)
                nc.scalar.activation(qk_sb[:, 0:DIM], dense[:, 0:DIM], ACT.Copy).then_inc(s_q_sb, 1)

            def read_k(t):
                act.wait_ge(s_k, t + 1)
                if not first(t):
                    act.wait_ge(s_cosm[1], t)
                    act.wait_ge(s_sinm[1], t)
                nc.scalar.activation(qk_sb[:, DIM:2 * DIM], dense[:, 512:1024], ACT.Copy).then_inc(s_k_sb, 1)

            def read_v(t):
                act.wait_ge(s_v, t + 1)
                if not first(t):
                    act.wait_ge(s_av[3], t)
                nc.scalar.activation(v_ext[:, :, 0:HD], score_b[:, 0:DIM].rearrange("p (h d) -> p h d", d=HD),
                                     ACT.Copy).then_inc(s_v_sb, 1)

            def split_hi(t, n):
                act.wait_ge(s_rot[n], t + 1)
                if not first(t):
                    act.wait_ge(s_tr[2 * n + 1], t)
                to = (q_parts[:, :, 0:3:2], k_parts[:, :, 0:2])[n]
                nc.scalar.activation(to, head_major(turned, n).unsqueeze(2).broadcast_to([P, HEADS, 2, HD]),
                                     ACT.Copy).then_inc(s_hi[n], 1)

            def read_qkT(t, n):
                act.wait_ge(s_tr[n], t + 1)
                if not first(t):
                    act.wait_ge(s_st[3], t)
                dst = (qT, qT, kT, kT)[n][:, (n % 2) * 1024:(n % 2 + 1) * 1024]
                src = dense[:, (n % 2) * 512:(n % 2 + 1) * 512].bitcast(f16)
                nc.scalar.activation(dst, src, ACT.Copy).then_inc(s_trr[n], 1)

            def read_neg_max(t):
                act.wait_ge(s_nmT, t + 1)
                if not first(t):
                    act.wait_ge(s_shift, t * 32)
                nc.scalar.activation(neg_maxT[:], score_a[:, 0:64].bitcast(f16), ACT.Copy).then_inc(s_nmT_sb, 1)

            def exp_group(t, g):
                act.wait_ge(s_st[g], t + 1)
                if g >= 2:
                    act.wait_ge(s_av[g - 2], t + 1)
                elif not first(t):
                    act.wait_ge(s_av[g + 2], t)
                nc.scalar.activation(probs[g % 2], scoreT_of[g][:], ACT.Exp).then_inc(s_ex[g], 1)

            def read_oT(t, n):
                act.wait_ge(s_av[2 * n + 1], t + 1)
                if not first(t):
                    act.wait_ge(s_o, t)
                nc.scalar.activation(oT_sb[:, n * 512:(n + 1) * 512], dense[:, n * 512:(n + 1) * 512],
                                     ACT.Copy).then_inc(s_oT[n], 1)

            def attn_hi(t):
                act.wait_ge(s_aT, t + 1)
                if not first(t):
                    act.wait_ge(s_proj, t)
                nc.scalar.activation(aT_h[:], gene[:, 0:DIM], ACT.Copy).then_inc(s_aT_h, 1)

            def y_hi(t):
                act.wait_ge(s_yT, t + 1)
                if not first(t):
                    act.wait_ge(s_lg[1], t)
                nc.scalar.activation(yT_h[:], gene[:, 0:DIM], ACT.Copy).then_inc(s_yT_h, 1)

            def read_logits(t, n):
                act.wait_ge(s_lg[n], t + 1)
                if not first(t):
                    act.wait_ge(s_rem[0], t)
                    act.wait_ge(s_gexp, t)
                nc.scalar.activation(logit[:, n * 512:(n + 1) * 512], gene[:, n * 512:(n + 1) * 512],
                                     ACT.Copy).then_inc(s_lgr[n], 1)

            def gene_exp(t):
                act.wait_ge(s_ntop, t + 1)
                if not first(t):
                    act.wait_ge(s_wT[1], t)
                nc.scalar.activation(gene_w, logit, ACT.Exp, bias=neg_top[:]).then_inc(s_gexp, 1)

            def read_wT(t, n):
                act.wait_ge(s_wT[n], t + 1)
                if not first(t):
                    act.wait_ge(s_eT, t)
                nc.scalar.activation(gene_wT[:, n * 512:(n + 1) * 512], gene[:, n * 512:(n + 1) * 512],
                                     ACT.Copy).then_inc(s_wTr[n], 1)

            def e_hi(t):
                act.wait_ge(s_eT, t + 1)
                if not first(t):
                    act.wait_ge(s_upp, t)
                nc.scalar.activation(eT_h[:], gene[:, 0:P], ACT.Copy).then_inc(s_eT_h, 1)

            def tanh(t):
                act.wait_ge(s_dn, t + 1)
                if not first(t):
                    act.wait_ge(s_y, t)
                act.wait_ge(s_ginv, t + 1)
                nc.scalar.activation(down[:], gene[:, 0:DIM], ACT.Tanh, scale=inv_gene_sum[:]).then_inc(s_tanh, 1)

            def iteration(l, a, b, c, d):
                if a is not None:
                    ctx_hi(a)
                    x_hi(a)
                if c is not None:
                    y_hi(c)
                if a is not None:
                    read_k(a)
                if b is not None:
                    read_neg_max(b)
                if c is not None:
                    read_logits(c, 0)
                    read_logits(c, 1)
                if a is not None:
                    read_q(a)
                if b is not None:
                    exp_group(b, 0)
                    exp_group(b, 1)
                if d is not None:
                    read_wT(d, 0)
                    read_wT(d, 1)
                if b is not None:
                    exp_group(b, 2)
                    read_oT(b, 0)
                    exp_group(b, 3)
                if d is not None:
                    e_hi(d)
                if a is not None:
                    split_hi(a, 0)
                if b is not None:
                    read_oT(b, 1)
                if a is not None:
                    split_hi(a, 1)
                if d is not None:
                    tanh(d)
                if a is not None:
                    read_qkT(a, 0)
                    read_qkT(a, 1)
                if b is not None:
                    attn_hi(b)
                if a is not None:
                    read_qkT(a, 2)
                if c is not None:
                    gene_exp(c)
                if a is not None:
                    read_qkT(a, 3)
                    read_v(a)

            filling = iteration

            def draining(l, a, b, c, d):
                if a is not None:
                    ctx_hi(a)
                    x_hi(a)
                    read_k(a)
                if c is not None:
                    y_hi(c)
                if a is not None:
                    read_q(a)
                if b is not None:
                    read_neg_max(b)
                if c is not None:
                    read_logits(c, 0)
                if a is not None:
                    split_hi(a, 0)
                if c is not None:
                    read_logits(c, 1)
                if b is not None:
                    exp_group(b, 0)
                    exp_group(b, 1)
                if d is not None:
                    read_wT(d, 0)
                    read_wT(d, 1)
                if b is not None:
                    exp_group(b, 2)
                    read_oT(b, 0)
                    exp_group(b, 3)
                if d is not None:
                    e_hi(d)
                if a is not None:
                    split_hi(a, 1)
                if b is not None:
                    read_oT(b, 1)
                if a is not None:
                    read_qkT(a, 0)
                if d is not None:
                    tanh(d)
                if a is not None:
                    read_qkT(a, 1)
                if b is not None:
                    attn_hi(b)
                if a is not None:
                    read_qkT(a, 2)
                    read_v(a)
                    read_qkT(a, 3)
                if c is not None:
                    gene_exp(c)

            def begin():
                ctx_hi(0)
                x_hi(0)
                read_k(0)
                wout_hi()
                read_q(0)
                read_v(0)
                wcT_hi(0)
                split_hi(0, 1)
                wcT_hi(1)
                wcT_hi(2)
                split_hi(0, 0)
                wcT_hi(3)
                duT_hi()
                for n in range(4):
                    read_qkT(0, n)

            run(act, begin, filling, iteration, draining)

        @block.vector
        def _(dve):
            steps = [0]

            def step(instruction):
                instruction.then_inc(s_setup, 1)
                steps[0] += 1
                dve.wait_ge(s_setup, steps[0])

            dve.wait_ge(s_posT, 1)
            by_freq = angle[:, 0].rearrange("p (t c j) -> p t c j", c=2, j=4)
            for j, freq in enumerate(ROPE_FREQS):
                last = nc.vector.tensor_scalar(by_freq[:, :, :, j],
                                               dense[:, 0:2 * TILES].rearrange("p (c t o) -> p (t o) c", c=2, o=1),
                                               freq, None, ALU.mult)
            step(last)
            step(nc.vector.tensor_scalar(turns, angle[:, 0], 1.0 / (TWO_PI_HI + TWO_PI_LO), None, ALU.mult))
            step(nc.vector.scalar_tensor_tensor(angle[:, 0], turns, -TWO_PI_HI, angle[:, 0], ALU.mult, ALU.add))
            step(nc.vector.scalar_tensor_tensor(angle[:, 0], turns, -TWO_PI_LO, angle[:, 0], ALU.mult, ALU.add))
            step(nc.vector.tensor_scalar(angle[:, 0], angle[:, 0], 3.1415925, -3.1415925, ALU.min, ALU.max))
            step(nc.vector.tensor_scalar(angle[:, 2], angle[:, 0], -1.0, None, ALU.mult))
            step(nc.vector.tensor_tensor(angle[:, 1], angle[:, 0], angle[:, 2], ALU.max))
            nc.vector.tensor_scalar(angle[:, 1], angle[:, 1], -1.0, 1.5707963, ALU.mult, ALU.add).then_inc(s_angle, 1)

            dve.wait_ge(s_ident, 1)
            nc.vector.tensor_copy(ident16[:], ident[:])
            nc.vector.memset(v_ext[:, :, HD:32], 0.0)
            nc.vector.memset(neg_max[:], 0.0)
            step(nc.vector.memset(parts[:, :, 3], 0.0))
            nc.vector.memset(k_parts[:, :, 3, 0:2], UNIT)
            nc.vector.memset(v_ext[:, :, HD:HD + 1], 1.0).then_inc(s_consts, 1)

            def scales():
                dve.wait_ge(s_small, 16 * 4)
                step(nc.vector.tensor_scalar(knob[:, 2:3], knob[:, 0:1], 0.1, None, ALU.max))
                step(nc.vector.reciprocal(knob[:, 2:3], knob[:, 2:3]))
                nc.vector.tensor_scalar(wc_scale[:], norm_sb[:], knob[:, 2:3], None, ALU.mult).then_inc(s_scales, 1)
                step(nc.vector.tensor_scalar(up_scale[:], norm_sb[:], knob[:, 1:2], None, ALU.mult))

            def scale_up():
                dve.wait_ge(s_du, 64)
                nc.vector.tensor_tensor(du_raw[:, 1], du_raw[:, 1],
                                        up_scale[:].unsqueeze(2).broadcast_to([P, XK, 2 * GD]),
                                        ALU.mult).then_inc(s_up, 1)

            def wout_lo():
                dve.wait_ge(s_wout_h, 1)
                nc.vector.tensor_tensor(wout_l[:].rearrange("p k n -> p (k n)"), wout_raw,
                                        wout_h[:].rearrange("p k n -> p (k n)").bitcast(f32),
                                        ALU.subtract).then_inc(s_split_out, 1)

            def wcT_lo(k):
                dve.wait_ge(s_wcT_h, k + 1)
                nc.vector.scalar_tensor_tensor(wcT_l[:, k], wcT_bank[k][:], wc_scale[:, k:k + 1],
                                               wcT_h[:, k].bitcast(f32), ALU.mult,
                                               ALU.subtract).then_inc(s_split_wcT, 1)

            def duT_lo():
                dve.wait_ge(s_duT_h, 1)
                nc.vector.tensor_tensor(wduT_l[:], score_b[0:GD, :], wduT_h[0:GD].bitcast(f32),
                                        ALU.subtract).then_inc(s_split_duT, 1)

            def norm1_stats(t):
                hold(dve)
                dve.wait_ge(s_x, (t + 1) * 16)
                nc.vector.bn_stats(bn1[:], slot(t)).then_inc(s_bn1, 1)
                hold(dve)
                dve.wait_ge(s_bn1, t + 1)
                nc.vector.bn_aggr(mv1[:], bn1[:]).then_inc(s_mv1, 1)
                dve.wait_ge(s_mv1, t + 1)
                nc.vector.tensor_scalar(var1[:], mv1[:, 1:2], LN_EPS, None, ALU.add).then_inc(s_var1, 1)

            def norm1_apply(t):
                dve.wait_ge(s_rstd1, t + 1)
                if not first(t):
                    dve.wait_ge(s_xT, t)
                nc.vector.tensor_scalar(xn[:], slot(t), mv1[:, 0:1], rstd1[:], ALU.subtract,
                                        ALU.mult).then_inc(s_xn, 1)

            def ctx_lo(t):
                dve.wait_ge(s_cT_h, t + 1)
                nc.vector.tensor_tensor(cT_l[:], dense[:, 512:512 + CTX], cT_h[:].bitcast(f32),
                                        ALU.subtract).then_inc(s_cT_l, 1)

            def x_lo(t):
                dve.wait_ge(s_xT_h, t + 1)
                nc.vector.tensor_tensor(xT_l[:], dense[:, 0:DIM], xT_h[:].bitcast(f32),
                                        ALU.subtract).then_inc(s_xT_l, 1)

            def group_max(t, g):
                dve.wait_ge(s_sc[g], t + 1)
                if g == 0 and not first(t):
                    dve.wait_ge(s_nml, t)
                nc.vector.tensor_reduce(row_max[:].rearrange("p (odd m) -> p odd m", odd=2)[:, :, 4 * g:4 * g + 4],
                                        score_of[g][:].rearrange("p (odd m k) -> p odd m k", odd=2, k=P),
                                        mybir.AxisListType.X, ALU.max).then_inc(s_mx[g], 1)

            def negate_max(t):
                high, low = (neg_max[:, 0:2 * HEADS].rearrange("p (odd l m) -> p l odd m", odd=2, l=2)[:, l]
                             for l in range(2))
                maxima = row_max[:].rearrange("p (odd m) -> p odd m", odd=2)
                for g in range(GROUPS):
                    dve.wait_ge(s_mx[g], t + 1)
                if not first(t):
                    dve.wait_ge(s_nmT, t)
                nc.vector.tensor_scalar(high, maxima, -1.0 / UNIT, None, ALU.mult).then_inc(s_nmh, 1)
                dve.wait_ge(s_nmh, t + 1)
                nc.vector.scalar_tensor_tensor(low, maxima, -1.0 / UNIT, high, ALU.mult, ALU.subtract).then_inc(s_nml, 1)

            def normalise(t):
                o = score_b[:].rearrange("p (h e) -> p h e", e=32)
                dve.wait_ge(s_o, t + 1)
                nc.vector.reciprocal(inv_sum[:].unsqueeze(2), o[:, :, HD:HD + 1]).then_inc(s_inv, 1)
                dve.wait_ge(s_inv, t + 1)
                if not first(t):
                    dve.wait_ge(s_aT, t)
                nc.vector.tensor_tensor(attn[:].rearrange("p (h d) -> p h d", d=HD), o[:, :, 0:HD],
                                        inv_sum[:].unsqueeze(2).broadcast_to([P, HEADS, HD]),
                                        ALU.mult).then_inc(s_attn, 1)

            def attn_lo(t):
                dve.wait_ge(s_aT_h, t + 1)
                nc.vector.tensor_tensor(aT_l[:], gene[:, 0:DIM], aT_h[:].bitcast(f32),
                                        ALU.subtract).then_inc(s_aT_l, 1)

            def residual(t):
                dve.wait_ge(s_proj, t + 1)
                dve.wait_ge(s_xb, t + 1)
                nc.vector.tensor_tensor(slot(t), gene[:, 512:1024], slot(t), ALU.add).then_inc(s_x1, 1)

            def norm2_stats(t):
                hold(dve)
                dve.wait_ge(s_x1, t + 1)
                nc.vector.bn_stats(bn2[:], slot(t)).then_inc(s_bn2, 1)
                hold(dve)
                dve.wait_ge(s_bn2, t + 1)
                nc.vector.bn_aggr(mv2[:], bn2[:]).then_inc(s_mv2, 1)
                dve.wait_ge(s_mv2, t + 1)
                nc.vector.tensor_scalar(var2[:], mv2[:, 1:2], 1.0 + RMS_EPS, RMS_EPS * LN_EPS, ALU.mult,
                                        ALU.add).then_inc(s_var2, 1)

            def norm2_apply(t):
                dve.wait_ge(s_norm2, t + 1)
                if not first(t):
                    dve.wait_ge(s_yT, t)
                nc.vector.tensor_scalar(yn[:], slot(t), mv2[:, 0:1], rstd2[:], ALU.subtract,
                                        ALU.mult).then_inc(s_yn, 1)

            def y_lo(t):
                dve.wait_ge(s_yT_h, t + 1)
                nc.vector.tensor_tensor(yT_l[:], gene[:, 0:DIM], yT_h[:].bitcast(f32),
                                        ALU.subtract).then_inc(s_yT_l, 1)

            def keep_norm(t):
                dve.wait_ge(s_norm2, t + 1)
                if not first(t):
                    dve.wait_ge(s_t2, t)
                nc.vector.tensor_copy(normx[:, 0:1], mv2[:, 0:1])
                nc.vector.tensor_copy(normx[:, 1:2], rstd2[:]).then_inc(s_normx, 1)

            def find_top(t, n):
                hold(dve)
                if n == 0:
                    dve.wait_ge(s_lgr[0], t + 1)
                    dve.wait_ge(s_lgr[1], t + 1)
                    if not first(t):
                        dve.wait_ge(s_rem[3], t)
                else:
                    dve.wait_ge(s_rem[n - 1], t + 1)
                nc.vector.max(top[:, 8 * n:8 * n + 8], logit if n == 0 else rest).then_inc(s_top[n], 1)

            def remove_top(t, n):
                hold(dve)
                dve.wait_ge(s_top[n], t + 1)
                if n == 0 and not first(t):
                    dve.wait_ge(s_gw, t)
                nc.vector.match_replace(rest, top[:, 8 * n:8 * n + 8], logit if n == 0 else rest,
                                        REMOVED).then_inc(s_rem[n], 1)

            def negate_top(t):
                dve.wait_ge(s_top[0], t + 1)
                if not first(t):
                    dve.wait_ge(s_gexp, t)
                nc.vector.tensor_scalar(neg_top[:], top[:, 0:1], -1.0, None, ALU.mult).then_inc(s_ntop, 1)

            def mask(t):
                dve.wait_ge(s_rem[3], t + 1)
                dve.wait_ge(s_gexp, t + 1)
                nc.vector.scalar_tensor_tensor(gene_w, rest, REMOVED, gene_w, ALU.is_equal, ALU.mult,
                                               accum_out=gene_sum[:]).then_inc(s_gw, 1)
                dve.wait_ge(s_gw, t + 1)
                if not first(t):
                    dve.wait_ge(s_tanh, t)
                nc.vector.reciprocal(inv_gene_sum[:], gene_sum[:]).then_inc(s_ginv, 1)
                dve.wait_ge(s_ginv, t + 1)
                dve.wait_ge(s_normx, t + 1)
                if not first(t):
                    dve.wait_ge(s_t2, t)
                nc.vector.tensor_tensor(up_factor[:], normx[:, 1:2], inv_gene_sum[:], ALU.mult).then_inc(s_upf, 1)

            def e_lo(t):
                dve.wait_ge(s_eT_h, t + 1)
                if not first(t):
                    dve.wait_ge(s_upp, t)
                nc.vector.tensor_copy(eT_hl[0:GD], eT_h[0:GD].bitcast(f32))
                nc.vector.tensor_tensor(eT_hl[GD:2 * GD], gene[GD:2 * GD, 0:P],
                                        eT_h[GD:2 * GD].bitcast(f32), ALU.subtract).then_inc(s_eT_l, 1)

            def combine(t):
                dve.wait_ge(s_tanh, t + 1)
                dve.wait_ge(s_normx, t + 1)
                nc.vector.scalar_tensor_tensor(down[:], slot(t), normx[:, 0:1], down[:], ALU.subtract,
                                               ALU.mult).then_inc(s_t1, 1)
                dve.wait_ge(s_t1, t + 1)
                dve.wait_ge(s_upp, t + 1)
                dve.wait_ge(s_upf, t + 1)
                nc.vector.scalar_tensor_tensor(down[:], down[:], up_factor[:], gene[:, 512:1024], ALU.mult,
                                               ALU.mult).then_inc(s_t2, 1)

            norm1_stats(0)
            norm1_apply(0)

            dve.wait_ge(s_wkv_h, 1)
            for k in range(CK):
                raw = wkv_raw[:, k * 1024:(k + 1) * 1024]
                nc.vector.tensor_tensor(wkv_l[:, k, 0:DIM].rearrange("p (two a) -> p two a", two=2),
                                        raw[:, 0:DIM].rearrange("p (a two) -> p two a", two=2),
                                        wkv_h[:, k, 0:DIM].bitcast(f32).rearrange("p (two a) -> p two a", two=2),
                                        ALU.subtract)
                last = nc.vector.tensor_tensor(wkv_l[:, k, DIM:1024], raw[:, DIM:1024],
                                               wkv_h[:, k, DIM:1024].bitcast(f32), ALU.subtract)
            last.then_inc(s_split_kv, 1)
            ctx_lo(0)
            dve.wait_ge(s_wq_h, 1)
            for k in range(XK):
                last = nc.vector.scalar_tensor_tensor(
                    wq_l[:, k].rearrange("p (two a) -> p two a", two=2),
                    wq_raw[:, k * DIM:(k + 1) * DIM].rearrange("p (a two) -> p two a", two=2), 0.25,
                    wq_h[:, k].bitcast(f32).rearrange("p (two a) -> p two a", two=2), ALU.mult, ALU.subtract)
            last.then_inc(s_split_q, 1)

            def iteration(l, a, b, c, d):
                if b is not None:
                    group_max(b, 0)
                if c is not None:
                    norm2_apply(c)
                if a is not None:
                    ctx_lo(a)
                if b is not None:
                    group_max(b, 1)
                if c is not None:
                    y_lo(c)
                if b is not None:
                    group_max(b, 2)
                    group_max(b, 3)
                    negate_max(b)
                if d is not None:
                    mask(d)
                if a is not None:
                    x_lo(a)
                if c is not None:
                    find_top(c, 0)
                    remove_top(c, 0)
                    find_top(c, 1)
                    negate_top(c)
                if l is not None:
                    norm1_stats(l)
                if c is not None:
                    remove_top(c, 1)
                    find_top(c, 2)
                if d is not None:
                    e_lo(d)
                if c is not None:
                    remove_top(c, 2)
                    find_top(c, 3)
                if b is not None:
                    normalise(b)
                if d is not None:
                    combine(d)
                if b is not None:
                    attn_lo(b)
                if c is not None:
                    remove_top(c, 3)
                    keep_norm(c)
                if l is not None:
                    norm1_apply(l)
                if b is not None:
                    residual(b)
                    norm2_stats(b)

            filling = iteration

            def draining(l, a, b, c, d):
                if a is not None:
                    ctx_lo(a)
                if b is not None:
                    group_max(b, 0)
                if c is not None:
                    norm2_apply(c)
                if b is not None:
                    group_max(b, 1)
                if a is not None:
                    x_lo(a)
                if b is not None:
                    group_max(b, 2)
                    group_max(b, 3)
                if c is not None:
                    y_lo(c)
                if b is not None:
                    negate_max(b)
                if d is not None:
                    mask(d)
                if c is not None:
                    find_top(c, 0)
                    remove_top(c, 0)
                    find_top(c, 1)
                    remove_top(c, 1)
                if d is not None:
                    e_lo(d)
                if c is not None:
                    find_top(c, 2)
                    negate_top(c)
                    remove_top(c, 2)
                if b is not None:
                    normalise(b)
                if d is not None:
                    combine(d)
                if b is not None:
                    attn_lo(b)
                if c is not None:
                    find_top(c, 3)
                    keep_norm(c)
                    remove_top(c, 3)
                if b is not None:
                    residual(b)
                    norm2_stats(b)

            def begin():
                x_lo(0)
                scales()
                norm1_stats(1)
                wcT_lo(0)
                scale_up()
                norm1_apply(1)
                wcT_lo(1)
                for k in range(2, 4):
                    wcT_lo(k)
                wout_lo()
                duT_lo()

            run(dve, begin, filling, iteration, draining)

        @block.tensor
        def _(pe):
            pe.wait_ge(s_ident, 1)
            pe.wait_ge(s_pos, 16)
            for c in range(2):
                last = nc.tensor.transpose(dense[:, c * TILES:(c + 1) * TILES], pos_raw[:, c:2 * P:2],
                                           ident[0:TILES, 0:TILES])
            last.then_inc(s_posT, 1)

            def wcT(k):
                pe.wait_ge(s_wc, 16)
                if k == 3:
                    pe.wait_ge(s_split_wcT, 1)
                for g in range(GK):
                    last = nc.tensor.transpose(wcT_bank[k][:, g * P:(g + 1) * P], wc_raw[:, g, k * P:(k + 1) * P], ident[:])
                last.then_inc(s_wcT, 1)

            def duT():
                pe.wait_ge(s_up, 1)
                pe.wait_ge(s_split_wcT, 2)
                for n in range(2):
                    for k in range(XK):
                        last = nc.tensor.transpose(score_b[:, n * DIM + k * P:n * DIM + (k + 1) * P],
                                                   du_raw[:, n, k], ident[:])
                last.then_inc(s_duT, 1)

            def three_pass(out, xs, ws, chunks):
                (xh, xl), (wh, wl) = xs, ws
                n, steps = 0, 3 * chunks
                for k in range(chunks):
                    for lhs, rhs in ((xh, wh), (xh, wl), (xl, wh)):
                        last = nc.tensor.matmul(out, lhs[:, k * P:(k + 1) * P], rhs(k), start=(n == 0),
                                                stop=(n == steps - 1))
                        n += 1
                return last

            def columns(w, at):
                return lambda k: w[:, k, at:at + 512]

            def transpose_x(t):
                pe.wait_ge(s_xn, t + 1)
                if not first(t):
                    pe.wait_ge(s_trr[2], t)
                for k in range(XK):
                    last = nc.tensor.transpose(dense[:, k * P:(k + 1) * P], xn[:, k * P:(k + 1) * P], ident[:])
                last.then_inc(s_xT, 1)

            def transpose_ctx(t):
                pe.wait_ge(s_ctx, (t + 1) * 16)
                if not first(t):
                    pe.wait_ge(s_trr[3], t)
                for k in range(CK):
                    last = nc.tensor.transpose(dense[:, 512 + k * P:512 + (k + 1) * P],
                                               ctx_sb[:, k * P:(k + 1) * P], ident[:])
                last.then_inc(s_cT, 1)

            def project_q(t):
                pe.wait_ge(s_xT_h, t + 1)
                pe.wait_ge(s_xT_l, t + 1)
                three_pass(dense[:, 0:512], (xT_h, xT_l), (columns(wq_h, 0), columns(wq_l, 0)),
                           XK).then_inc(s_q, 1)

            def project_k(t):
                pe.wait_ge(s_cT_h, t + 1)
                pe.wait_ge(s_cT_l, t + 1)
                three_pass(dense[:, 512:1024], (cT_h, cT_l), (columns(wkv_h, 0), columns(wkv_l, 0)),
                           CK).then_inc(s_k, 1)

            def project_v(t):
                if not first(t):
                    pe.wait_ge(s_attn, t)
                three_pass(score_b[:, 0:512], (cT_h, cT_l), (columns(wkv_h, 512), columns(wkv_l, 512)),
                           CK).then_inc(s_v, 1)

            def transpose_qk(t, n):
                if n == 0:
                    pe.wait_ge(s_hi[0], t + 1)
                    pe.wait_ge(s_lo[0], t + 1)
                    pe.wait_ge(s_q_sb, t + 1)
                    if not first(t):
                        pe.wait_ge(s_oT[0], t)
                elif n == 1:
                    pe.wait_ge(s_k_sb, t + 1)
                    if not first(t):
                        pe.wait_ge(s_oT[1], t)
                else:
                    if n == 2:
                        pe.wait_ge(s_hi[1], t + 1)
                        pe.wait_ge(s_lo[1], t + 1)
                    pe.wait_ge(s_trr[n - 2], t + 1)
                half = dense[:, (n % 2) * 512:(n % 2 + 1) * 512].bitcast(f16)
                for m in range(8):
                    last = nc.tensor.transpose(half[:, m * P:(m + 1) * P],
                                               pair_in(n // 2, (n % 2) * 8 + m), ident16[:])
                last.then_inc(s_tr[n], 1)

            def scores(t, g):
                if g == 0:
                    for n in range(4):
                        pe.wait_ge(s_trr[n], t + 1)
                    if not first(t):
                        pe.wait_ge(s_ex[3], t)
                elif g == 1:
                    pe.wait_ge(s_v_sb, t + 1)
                else:
                    pe.wait_ge(s_mx[g - 2], t + 1)
                for r in range(GH):
                    head = g * GH + r
                    at = (r % 2) * 512 + (r // 2) * P
                    last = nc.tensor.matmul(score_of[g][:, at:at + P], rows_of(qT, head), rows_of(kT, head),
                                            start=True, stop=True)
                last.then_inc(s_sc[g], 1)

            def transpose_neg_max(t):
                pe.wait_ge(s_nmh, t + 1)
                pe.wait_ge(s_nml, t + 1)
                nc.tensor.transpose(score_a[:, 0:64].bitcast(f16), neg_max[:], ident16[:]).then_inc(s_nmT, 1)

            def scoresT(t, g):
                if g == 0:
                    pe.wait_ge(s_shift, (t + 1) * 32)
                elif g >= 2:
                    pe.wait_ge(s_ex[g - 2], t + 1)
                for r in range(GH):
                    head = g * GH + r
                    at = (r % 2) * 512 + (r // 2) * P
                    last = nc.tensor.matmul(scoreT_of[g][:, at:at + P], rows_of(kT, head), rows_of(qT, head),
                                            start=True, stop=True)
                last.then_inc(s_st[g], 1)

            def values(t, g):
                if g == 0:
                    pe.wait_ge(s_v_sb, t + 1)
                    if not last_tile(t):
                        pe.wait_ge(s_q_sb, t + 2)
                elif g == 2 and not last_tile(t):
                    pe.wait_ge(s_k_sb, t + 2)
                pe.wait_ge(s_ex[g], t + 1)
                for r in range(GH):
                    head = g * GH + r
                    rows = slice(32 * (r % 4), 32 * (r % 4) + 32)
                    at = (2 * g + r // 4) * P
                    slot_at = ((r % 2) * 4 + r // 2) * P
                    last = nc.tensor.matmul(dense[rows, at:at + P], v_ext[:, head], probs[g % 2][:, slot_at:slot_at + P],
                                            start=True, stop=True)
                last.then_inc(s_av[g], 1)

            def transpose_o(t):
                pe.wait_ge(s_oT[0], t + 1)
                pe.wait_ge(s_oT[1], t + 1)
                pe.wait_ge(s_ex[2], t + 1)
                for n in range(8):
                    last = nc.tensor.transpose(score_b[:, n * P:(n + 1) * P], oT_sb[:, n * P:(n + 1) * P], ident[:])
                last.then_inc(s_o, 1)

            def transpose_attn(t):
                pe.wait_ge(s_attn, t + 1)
                if not isinstance(t, int) or t >= 2:
                    pe.wait_ge(s_tanh, t - 1)
                for k in range(XK):
                    last = nc.tensor.transpose(gene[:, k * P:(k + 1) * P], attn[:, k * P:(k + 1) * P], ident[:])
                last.then_inc(s_aT, 1)

            def project_out(t):
                pe.wait_ge(s_aT_h, t + 1)
                pe.wait_ge(s_aT_l, t + 1)
                if not isinstance(t, int) or t >= 2:
                    pe.wait_ge(s_t2, t - 1)
                three_pass(gene[:, 512:1024], (aT_h, aT_l), (columns(wout_h, 0), columns(wout_l, 0)),
                           XK).then_inc(s_proj, 1)

            def transpose_y(t):
                pe.wait_ge(s_yn, t + 1)
                for k in range(XK):
                    last = nc.tensor.transpose(gene[:, k * P:(k + 1) * P], yn[:, k * P:(k + 1) * P], ident[:])
                last.then_inc(s_yT, 1)

            def logits(t, n):
                if n == 0:
                    pe.wait_ge(s_yT_h, t + 1)
                    pe.wait_ge(s_yT_l, t + 1)
                three_pass(gene[:, n * 512:(n + 1) * 512], (yT_h, yT_l),
                           (columns(wcT_h, n * 512), columns(wcT_l, n * 512)), XK).then_inc(s_lg[n], 1)

            def transpose_w(t, n):
                pe.wait_ge(s_gw, t + 1)
                if last_tile(t):
                    pe.wait_ge((s_tanh, s_t2)[n], t)
                else:
                    pe.wait_ge(s_lgr[n], t + 2)
                for g in range(4 * n, 4 * n + 4):
                    last = nc.tensor.transpose(gene[:, g * P:(g + 1) * P], gene_w[:, g * P:(g + 1) * P], ident[:])
                last.then_inc(s_wT[n], 1)

            def express(t):
                pe.wait_ge(s_wTr[0], t + 1)
                pe.wait_ge(s_wTr[1], t + 1)
                for g in range(GK):
                    last = nc.tensor.matmul(gene[:, 0:P], genes_sb[:, g], gene_wT[:, g * P:(g + 1) * P],
                                            start=(g == 0), stop=(g == GK - 1))
                last.then_inc(s_eT, 1)

            def down_up(t):
                pe.wait_ge(s_eT_h, t + 1)
                pe.wait_ge(s_eT_l, t + 1)
                for n, done in enumerate((s_dn, s_upp)):
                    cols = slice(n * DIM, (n + 1) * DIM)
                    nc.tensor.matmul(gene[:, cols], eT_hl[:], wduT_h[:, cols], start=True, stop=False)
                    nc.tensor.matmul(gene[:, cols], eT_h[0:GD], wduT_l[:, cols], start=False,
                                     stop=True).then_inc(done, 1)

            def iteration(l, a, b, c, d):
                if b is not None:
                    scores(b, 0)
                    scores(b, 1)
                if a is not None:
                    transpose_ctx(a)
                    transpose_x(a)
                if b is not None:
                    scores(b, 2)
                if c is not None:
                    transpose_y(c)
                if a is not None:
                    project_k(a)
                if b is not None:
                    scores(b, 3)
                if c is not None:
                    logits(c, 0)
                if b is not None:
                    transpose_neg_max(b)
                if c is not None:
                    logits(c, 1)
                if a is not None:
                    project_q(a)
                if b is not None:
                    scoresT(b, 0)
                if d is not None:
                    transpose_w(d, 0)
                if b is not None:
                    scoresT(b, 1)
                if d is not None:
                    transpose_w(d, 1)
                if b is not None:
                    values(b, 0)
                    scoresT(b, 2)
                    values(b, 1)
                    scoresT(b, 3)
                if d is not None:
                    express(d)
                if b is not None:
                    values(b, 2)
                    values(b, 3)
                if d is not None:
                    down_up(d)
                if b is not None:
                    transpose_o(b)
                if a is not None:
                    transpose_qk(a, 0)
                    transpose_qk(a, 1)
                if b is not None:
                    transpose_attn(b)
                if a is not None:
                    transpose_qk(a, 2)
                    transpose_qk(a, 3)
                if b is not None:
                    project_out(b)
                if a is not None:
                    project_v(a)

            filling = iteration

            def draining(l, a, b, c, d):
                if a is not None:
                    transpose_ctx(a)
                    transpose_x(a)
                if b is not None:
                    scores(b, 0)
                    scores(b, 1)
                if a is not None:
                    project_k(a)
                if b is not None:
                    scores(b, 2)
                if c is not None:
                    transpose_y(c)
                if b is not None:
                    scores(b, 3)
                if a is not None:
                    project_q(a)
                if b is not None:
                    transpose_neg_max(b)
                if c is not None:
                    logits(c, 0)
                    logits(c, 1)
                if b is not None:
                    scoresT(b, 0)
                if d is not None:
                    transpose_w(d, 0)
                if b is not None:
                    scoresT(b, 1)
                if d is not None:
                    transpose_w(d, 1)
                if b is not None:
                    values(b, 0)
                    scoresT(b, 2)
                    values(b, 1)
                    scoresT(b, 3)
                if d is not None:
                    express(d)
                if b is not None:
                    values(b, 2)
                if a is not None:
                    transpose_qk(a, 0)
                if b is not None:
                    values(b, 3)
                if d is not None:
                    down_up(d)
                if b is not None:
                    transpose_o(b)
                if a is not None:
                    transpose_qk(a, 1)
                    transpose_qk(a, 2)
                if b is not None:
                    transpose_attn(b)
                if a is not None:
                    project_v(a)
                    transpose_qk(a, 3)
                if b is not None:
                    project_out(b)

            def begin():
                transpose_ctx(0)
                transpose_x(0)
                pe.wait_ge(s_consts, 1)
                pe.wait_ge(s_split_kv, 1)
                project_k(0)
                pe.wait_ge(s_split_q, 1)
                project_q(0)
                project_v(0)
                wcT(0)
                pe.wait_ge(s_v_sb, 1)
                wcT(1)
                wcT(2)
                wcT(3)
                duT()
                for n in range(4):
                    transpose_qk(0, n)
                pe.wait_ge(s_genes, 32)
                pe.wait_ge(s_split_out, 1)
                pe.wait_ge(s_split_wcT, 4)
                pe.wait_ge(s_split_duT, 1)

            run(pe, begin, filling, iteration, draining)


NAMES = ['x', 'ctx_1024', 'fside_BxSx2_0', 'L0_xattn_Wq', 'L0_xattn_Wkv', 'L0_xattn_Wout', 'L0_xattn_bout',
         'L0_ffn_Wc', 'L0_ffn_temperature', 'L0_ffn_genes', 'L0_ffn_Wd', 'L0_ffn_Wu', 'L0_ffn_norm_w',
         'L0_ffn_scale']


def kernel(**inputs):
    import numpy as np
    import concourse.bacc as bacc
    from concourse.bass_utils import run_bass_kernel_spmd

    nc = bacc.Bacc("TRN2", target_bir_lowering=False, num_devices=1)
    arrays, args = {}, []
    for name in NAMES:
        a = np.ascontiguousarray(inputs[name])
        a = a.reshape(a.shape or (1,))
        if name == 'L0_ffn_norm_w':
            a = np.ascontiguousarray(a.reshape(XK, P).T)
        arrays[name + "_dram"] = a
        args.append(nc.dram_tensor(name + "_dram", a.shape, mybir.dt.from_np(a.dtype), kind="ExternalInput").ap())
    out = nc.dram_tensor("out_dram", (TILES, P, DIM), f32, kind="ExternalOutput").ap()
    build(nc, *args, out)
    result = run_bass_kernel_spmd(nc, [arrays], core_ids=[0])
    return result.results[0]["out_dram"]
```
